# Optimizing a Trainium2 kernel written in Bass

```python
import numpy as np
import jax
import jax.numpy as jnp

def _softmax(x, axis=-1):
    return jax.nn.softmax(x, axis=axis)

def _gelu(x):
    return jax.nn.gelu(x, approximate=True)

def _silu(x):
    return jax.nn.silu(x)

def _sigmoid(x):
    return jax.nn.sigmoid(x)

def _layernorm(x, axis=-1, eps=1e-05):
    m = jnp.mean(x, axis=axis, keepdims=True)
    v = jnp.var(x, axis=axis, keepdims=True)
    return (x - m) / jnp.sqrt(v + eps)

def _scatter_add(tgt, idx, src, axis=0):
    return tgt.at[idx].add(src)

def _segment_sum(src, seg, n):
    return jax.ops.segment_sum(src, seg, n)
kernel_name = 'mk_adj_preln_d2_adj_r2_c1e627'

def setup_inputs(seed: int=0):
    np.random.seed(seed)
    _w = jnp.asarray

    def _rec_inputs():
        import jax
        import jax.numpy as jnp
        _gk = jax.random.key(seed)
        x = -0.000929 + 1 * jax.random.normal(jax.random.fold_in(_gk, 1), (8192, 128), jnp.float32)
        _w = (1.0 + jnp.arange(8192, dtype=jnp.float32)) ** (-0.5)
        _w = _w / _w.mean()
        _pij = jnp.clip(0.000244141 * _w[:, None] * _w[None, :], 0.0, 1.0)
        _a = jax.random.uniform(jax.random.fold_in(_gk, 2), (8192, 8192)) < _pij
        adj = _a.astype(jnp.int32)
        return (x, adj)
    x, adj = _rec_inputs()

    def _L0_gnn_setup():
        import jax, jax.numpy as jnp
        import numpy as np
        NEG_INF = -1000000000.0
        key = jax.random.key(seed)
        k1, k2, k3, k4 = jax.random.split(key, 4)
        N, Fin, Fout = (4096, 128, 128)
        h = jax.random.normal(k1, (N, Fin), dtype=jnp.float32)
        adj = jax.random.randint(k2, (N, N), 0, 2, dtype=jnp.int32)
        W = jax.random.normal(k3, (Fin, Fout), dtype=jnp.float32) * (1.0 / np.sqrt(Fin))
        a = jax.random.normal(k4, (2 * Fout,), dtype=jnp.float32) * (1.0 / np.sqrt(2 * Fout))
        return {'h': h, 'adj': adj, 'W': W, 'a': a}
    _L0_gnn_all = _L0_gnn_setup()
    _L0_gnn_in = {k: v for k, v in _L0_gnn_all.items() if k in ('W', 'a')}
    del _L0_gnn_all

    def _L1_gnn_setup():
        import jax, jax.numpy as jnp
        import numpy as np
        N = 4096
        D_IN = 128
        D_OUT = 128
        ALPHA = 0.2
        NEG = -9000000000000000.0
        key = jax.random.key(seed)
        k1, k2, k3, k4 = jax.random.split(key, 4)
        input = jax.random.normal(k1, (N, D_IN), dtype=jnp.float32)
        adj = jax.random.randint(k2, (N, N), 0, 2, dtype=jnp.int32)
        lim_w = 1.414 * np.sqrt(6.0 / (D_IN + D_OUT))
        W = jax.random.uniform(k3, (D_IN, D_OUT), jnp.float32, -lim_w, lim_w)
        lim_a = 1.414 * np.sqrt(6.0 / (2 * D_OUT + 1))
        a = jax.random.uniform(k4, (2 * D_OUT, 1), jnp.float32, -lim_a, lim_a)
        return {'input': input, 'adj': adj, 'W': W, 'a': a}
    _L1_gnn_all = _L1_gnn_setup()
    _L1_gnn_in = {k: v for k, v in _L1_gnn_all.items() if k in ('W', 'a')}
    del _L1_gnn_all
    return {'x': x, 'adj': adj, 'L0_gnn_W': _L0_gnn_in['W'], 'L0_gnn_a': _L0_gnn_in['a'], 'L1_gnn_W': _L1_gnn_in['W'], 'L1_gnn_a': _L1_gnn_in['a']}

def reference(x, adj, L0_gnn_W, L0_gnn_a, L1_gnn_W, L1_gnn_a):
    import jax
    import jax.numpy as jnp

    def _L0_gnn_ref(h, adj, W, a):
        import jax, jax.numpy as jnp
        import numpy as np
        NEG_INF = -1000000000.0
        Fout = W.shape[1]
        Wh = h @ W
        a1, a2 = (a[:Fout], a[Fout:])
        s_key = Wh @ a1
        s_qry = Wh @ a2
        e = jax.nn.leaky_relu(s_qry[:, None] + s_key[None, :], negative_slope=0.2)
        scores = jnp.where(adj > 0, e, jnp.float32(NEG_INF))
        attention = jax.nn.softmax(scores, axis=1)
        h_prime = attention @ Wh
        return jax.nn.elu(h_prime)

    def _L1_gnn_ref(input, adj, W, a):
        import jax, jax.numpy as jnp
        import numpy as np
        N = 4096
        D_IN = 128
        D_OUT = 128
        ALPHA = 0.2
        NEG = -9000000000000000.0
        h = input @ W
        a1 = a[:D_OUT, 0]
        a2 = a[D_OUT:, 0]
        e = (h @ a1)[:, None] + (h @ a2)[None, :]
        e = jnp.where(e > 0, e, ALPHA * e)
        e = jnp.where(adj > 0, e, NEG)
        attention = jax.nn.softmax(e, axis=1)
        h_prime = attention @ h
        return jax.nn.elu(h_prime)
    h = jnp.maximum(_layernorm(x, axis=-1), 0.0)
    x = x + _L0_gnn_ref(h, adj, L0_gnn_W, L0_gnn_a)
    h = jnp.maximum(_layernorm(x, axis=-1), 0.0)
    x = x + _L1_gnn_ref(h, adj, L1_gnn_W, L1_gnn_a)
    return x

_drawn_inputs = setup_inputs


def setup_inputs(seed=0):
    import zlib

    import numpy as np

    out = dict(_drawn_inputs(seed))
    spreads = {}
    factors = {}
    for name, (base, spread) in spreads.items():
        noise = np.random.default_rng([zlib.crc32(name.encode()), seed]).standard_normal(out[name].shape)
        drawn = base * np.exp(spread * noise) if base else spread * noise
        out[name] = jnp.asarray(drawn.astype(out[name].dtype))
    for name, factor in factors.items():
        out[name] = (out[name] * factor).astype(out[name].dtype)
    return out
```

```python
from contextlib import ExitStack

import numpy as np
import concourse.bass as bass
from concourse import mybir
from concourse.alu_op_type import AluOpType as ALU

ACT = mybir.ActivationFunctionType
AX = mybir.AxisListType
F32 = mybir.dt.float32
BF16 = mybir.dt.bfloat16
I32 = mybir.dt.int32
U16 = mybir.dt.uint16

P = 128
WORD = 16
NW = P // WORD
G = 8
CH = 4
EPS = 1e-5
ALPHA = 0.2
MASKED = -1e30
FLOOR = -1e28
BLOCK_CODE = 1 << WORD


class Chain:

    def __init__(self, eng, sem):
        self.eng, self.sem, self.n = eng, sem, 0

    def done(self, ins):
        ins.then_inc(self.sem, 1)
        self.n += 1

    def wait(self):
        self.eng.wait_ge(self.sem, self.n)

    def link(self, ins):
        self.done(ins)
        self.wait()

    def restart(self):
        if self.n:
            self.wait()
            self.eng.sem_clear(self.sem)
            self.n = 0


def gat_two_layers(nc, x, adj, W0, a0, W1, a1, ident_c, code_c, bitmask_c, block_c, lane_c, out):
    N, F = x.shape
    T = N // P
    T2 = T // 2
    NC2 = T // CH // 2
    LD = 4
    LW = N // LD
    LB = LW // P
    VW = F + 3
    QC, KC, ONE = F, F + 1, F + 2
    VS = VW + 1
    GW = G * P
    RND = T // G

    table = nc.dram_tensor("value_table", [N, VS], F32, kind="Internal").ap()
    x1 = nc.dram_tensor("x_between_layers", [N, F], F32, kind="Internal").ap()
    layer_in, layer_out = [x, x1], [x1, out]

    with ExitStack() as ctx:
        def sb(name, shape, dt=F32):
            return ctx.enter_context(nc.sbuf_tensor(name, shape, dt))

        def sem(name):
            return ctx.enter_context(nc.semaphore(name))

        def sem2(name):
            return [sem(f"{name}{i}") for i in range(2)]

        ident = sb("ident", [P, P])
        ones = sb("ones", [P, P])
        code_f = sb("code_f", [P, NW])
        code = sb("code", [P, NW], BF16)
        bitmask = sb("bitmask", [P, P], U16)
        blockcode = sb("blockcode", [P, T])
        lane = sb("lane", [P, 1])
        Wx = [sb(f"Wx{l}", [P, F + 2]) for l in range(2)]
        acol = [sb(f"acol{l}", [P, 2]) for l in range(2)]
        WT = sb("WT", [P, P])
        xin = sb("xin", [P, 2, CH, F])
        cen = sb("cen", [P, CH, F])
        sq = sb("sq", [P, CH, F])
        stat = sb("stat", [P, 4, CH])
        hrow = sb("hrow", [P, 2, CH, F])
        hT = sb("hT", [P, 2, CH * P])
        vrow = sb("vrow", [P, 2, CH, VS])
        vsum = sb("vsum", [P, CH, VS])
        qcol = sb("qcol", [P, T])
        sumrep = sb("sumrep", [P, VS])
        adj_in = sb("adj_in", [P, LD, LW], I32)
        a01 = sb("a01", [P, 2, LW], BF16)
        occ = sb("occ", [P, T])
        occ01 = sb("occ01", [P, T])
        base = sb("base", [P, T])
        cnt = sb("cnt", [P, 2])
        codes = sb("codes", [P, NW, T])
        top = sb("top", [P, NW, G])
        topi = sb("topi", [P, NW, G], I32)
        blk = sb("blk", [P, G])
        nmax = sb("nmax", [1, 1])
        words = sb("words", [P, T * T * NW], U16)
        idx = sb("idx", [P, T * T], U16)
        nslots = sb("nslots", [1, T], I32)
        nlast = sb("nlast", [1, T], I32)
        idxs = sb("idxs", [P, 2, G], I32)
        rows = sb("rows", [P, 2, G, VS])
        bits = sb("bits", [P, GW], U16)
        sc = sb("sc", [P, 2, GW])
        pr = sb("pr", [P, 2, GW])
        kr = sb("kr", [P, 2, P])
        qb = sb("qb", [P, 2, P])
        mb = sb("mb", [P, 2, P])
        col = sb("col", [P, 2, 8])
        acc = sb("acc", [P, 2, VW])
        fcol = sb("fcol", [P, 2, 4])
        num = sb("num", [P, 2, F])
        hmin = sb("hmin", [P, 2, F])
        xres = sb("xres", [P, 2, F])
        obuf = sb("obuf", [P, 2, F])

        ps = ctx.enter_context(nc.psum_tensor("ps", [P, 8, 512], F32))

        s_const, s_memset, s_W, s_init = sem("s_const"), sem("s_memset"), sem("s_W"), sem("s_init")
        s_wt, s_wts, s_wa, s_was = sem("s_wt"), sem("s_wts"), sem("s_wa"), sem("s_was")
        s_var, s_std = sem2("s_var"), sem2("s_std")
        s_xin, s_h, s_hT, s_hTs = sem2("s_xin"), sem2("s_h"), sem2("s_hT"), sem2("s_hTs")
        s_wh, s_vrow, s_q, s_vs, s_tab = sem2("s_wh"), sem2("s_vrow"), sem2("s_q"), sem2("s_vs"), sem2("s_tab")
        s_sum, s_sumrep = sem("s_sum"), sem("s_sumrep")
        s_adj = [sem(f"s_adj{i}") for i in range(LD)]
        s_conv = [sem(f"s_conv{i}") for i in range(LD)]
        s_pack, s_code, s_cnt, s_cntT = sem2("s_pack"), sem2("s_code"), sem2("s_cnt"), sem2("s_cntT")
        s_packed = sem("s_packed")
        s_idx, s_rows, s_kr, s_kT = sem2("s_idx"), sem2("s_rows"), sem2("s_kr"), sem2("s_kT")
        s_qb, s_qrep, s_mb, s_mrep = sem2("s_qb"), sem2("s_qrep"), sem2("s_mb"), sem2("s_mrep")
        s_d, s_p, s_pv = sem2("s_d"), sem2("s_p"), sem2("s_pv")
        s_dm, s_corr, s_acc = sem2("s_dm"), sem2("s_corr"), sem2("s_acc")
        s_hmin, s_em, s_fin, s_xres, s_out = sem2("s_hmin"), sem2("s_em"), sem2("s_fin"), sem2("s_xres"), sem2("s_out")
        s_held = sem("s_held")
        s_vchain, s_gchain = sem("s_vchain"), sem("s_gchain")

        def chunk(dram, c):
            return dram[bass.ds(c * (CH * P), CH * P), :].rearrange("(q p) f -> p q f", p=P)

        def credit(eng, *sems):
            for s in sems:
                eng.sem_inc(s, 1)

        def hold(eng, s, value):
            eng.wait_ge(s, value)
            eng.sem_inc(s_held, 1)

        block = ctx.enter_context(nc.Block())

        @block.sync
        def _(sp):
            for dst, src in ((ident, ident_c), (code_f, code_c), (bitmask, bitmask_c), (blockcode, block_c),
                             (lane, lane_c)):
                sp.dma_start(dst[:, :], src).then_inc(s_const, 16)
            for l, (W, a) in enumerate(((W0, a0), (W1, a1))):
                sp.dma_start(Wx[l][:, 0:F], W).then_inc(s_W, 16)
                with nc.allow_non_contiguous_dma(reason="256 numbers"):
                    sp.dma_start(acol[l][:, :], a.rearrange("(s p) -> p s", p=P)).then_inc(s_W, 16)

            def load_x(layer):
                with sp.Fori(0, NC2) as cc:
                    for b in range(2):
                        sp.wait_ge(s_h[b], layer * NC2 + cc + 1)
                        sp.dma_start(xin[:, b], chunk(layer_in[layer], 2 * cc + b)).then_inc(s_xin[b], 16)
                        if b == 1:
                            store_values(layer, cc)

            def store_values(layer, cc):
                for b in range(2):
                    sp.wait_ge(s_vrow[b], layer * NC2 + cc + 2)
                    sp.dma_start(chunk(table, 2 * cc + b), vrow[:, b]).then_inc(s_tab[b], 16)

            def load_adj():
                with sp.Fori(0, T2) as tt:
                    for b in range(2):
                        t = 2 * tt + b
                        for k in range(LD):
                            sp.wait_ge(s_conv[k], t + 1)
                            sp.dma_start(adj_in[:, k], adj[bass.ds(t * P, P), k * LW:(k + 1) * LW]).then_inc(s_adj[k], 16)

            def residual_and_store(layer):
                with sp.Fori(0, T2) as tt:
                    n = layer * T2 + tt
                    for b in range(2):
                        sp.wait_ge(s_fin[b], n + 1)
                        sp.dma_start(xres[:, b], layer_in[layer][bass.ds((2 * tt + b) * P, P), :]).then_inc(s_xres[b], 16)
                    for b in range(2):
                        sp.wait_ge(s_fin[b], n + 2)
                        sp.dma_start(layer_out[layer][bass.ds((2 * tt + b) * P, P), :], obuf[:, b]).then_inc(s_out[b], 16)
                for b in range(2):
                    sp.wait_ge(s_out[b], 16 * T2 * (layer + 1))

            load_x(0)
            load_adj()
            residual_and_store(0)
            load_x(1)
            residual_and_store(1)

        @block.gpsimd
        def _(pool):
            chain = Chain(pool, s_gchain)
            unit = [pool.alloc_register(f"pool_unit{b}") for b in range(2)]
            for b in range(2):
                pool.reg_mov(unit[b], 1)

            def sum_values(layer):
                chain.link(pool.memset(vsum[:, :, :], 0.0))
                chain.restart()
                with pool.Fori(0, NC2) as cc:
                    for b in range(2):
                        pool.wait_ge(s_vrow[b], layer * NC2 + cc + 2)
                        ins = pool.tensor_tensor(vsum[:, :, 0:VW], vsum[:, :, 0:VW], vrow[:, b, :, 0:VW], ALU.add)
                        chain.link(ins)
                        pool.sem_inc(s_vs[b], 1)
                    chain.restart()

            def gather(layer):
                for b in range(2):
                    pool.wait_ge(s_tab[b], 16 * NC2 * (layer + 1))
                with pool.Fori(0, T2) as tt:
                    for b in range(2):
                        t = 2 * tt + b
                        n = pool.value_load(nslots[0:1, bass.ds(t, 1)], min_val=1, max_val=T)
                        with pool.Fori(0, (n + G - 1) // G) as g:
                            u = pool.snap(unit[b])
                            pool.wait_ge(s_pv[b], u)
                            pool.tensor_copy(idxs[:, b, :], idx[:, bass.ds(t * T + g * G, G)]).then_inc(s_idx[b], 1)
                            hold(pool, s_idx[b], u)
                            for s in range(G):
                                with pool.If(n > g * G + s):
                                    pool.indirect_dma_start(
                                        out=rows[:, b, s, :], out_offset=None, in_=table[:, :],
                                        in_offset=bass.IndirectOffsetOnAxis(ap=idxs[:, b, s:s + 1], axis=0),
                                    ).then_inc(s_rows[b], 16)
                            pool.reg_add(unit[b], unit[b], 1)

            credit(pool, *s_vs)
            pool.wait_ge(s_init, 1)
            sum_values(0)
            pool.wait_ge(s_packed, 1)
            gather(0)
            sum_values(1)
            gather(1)

        @block.scalar
        def _(act):
            unit = [act.alloc_register(f"act_unit{b}") for b in range(2)]
            for b in range(2):
                act.reg_mov(unit[b], 1)

            def project(layer):
                with act.Fori(0, NC2) as cc:
                    c = layer * NC2 + cc
                    for b in range(2):
                        act.wait_ge(s_var[b], c + 1)
                        act.activation(stat[:, 2, :], stat[:, 2, :], ACT.Sqrt).then_inc(s_std[b], 1)
                        act.wait_ge(s_hT[b], c + 2)
                        act.activation(hT[:, b, :], ps[:, b, :], ACT.Copy).then_inc(s_hTs[b], 1)
                        with act.If(c > 0):
                            hold(act, s_tab[b], 16 * c)
                        act.wait_ge(s_wh[b], c + 1)
                        act.wait_ge(s_vs[b], c + 1)
                        act.wait_ge(s_q[b], c + 1)
                        wh = ps[:, 2 + 2 * b:4 + 2 * b, :].rearrange("p k (h w) -> p (k h) w", h=2)
                        act.activation(vrow[:, b, :, 0:F + 2], wh[:, :, 0:F + 2], ACT.Copy).then_inc(s_vrow[b], 1)
                        act.wait_ge(s_vrow[b], c + 2)
                        act.activation(qcol[:, bass.ds((2 * cc + b) * CH, CH)], vrow[:, b, :, QC], ACT.Copy).then_inc(s_q[b], 1)

            def attend(layer):
                with act.Fori(0, T2) as tt:
                    for b in range(2):
                        t = 2 * tt + b
                        n = act.value_load(nslots[0:1, bass.ds(t, 1)], min_val=1, max_val=T)
                        with act.Fori(0, (n + G - 1) // G) as g:
                            u = act.snap(unit[b])
                            act.wait_ge(s_dm[b], u)
                            act.activation(col[:, b, 6:7], col[:, b, 5:6], ACT.Exp).then_inc(s_corr[b], 1)
                            act.wait_ge(s_d[b], u)
                            act.wait_ge(s_pv[b], u)
                            act.activation(pr[:, b, :], sc[:, b, :], ACT.Exp).then_inc(s_p[b], 1)
                            act.reg_add(unit[b], unit[b], 1)
                        act.wait_ge(s_hmin[b], layer * T2 + tt + 1)
                        act.activation(hmin[:, b, :], hmin[:, b, :], ACT.Exp).then_inc(s_em[b], 1)

            credit(act, *s_hTs, *s_vrow, *s_q)
            project(0)
            act.wait_ge(s_packed, 1)
            attend(0)
            project(1)
            attend(1)

        @block.vector
        def _(dve):
            chain = Chain(dve, s_vchain)
            unit = [dve.alloc_register(f"dve_unit{b}") for b in range(2)]
            gathered = [dve.alloc_register(f"dve_gathered{b}") for b in range(2)]
            for b in range(2):
                dve.reg_mov(gathered[b], 0)
                dve.reg_mov(unit[b], 1)

            def init():
                dve.memset(ones[:, :], 1.0).then_inc(s_memset, 1)
                chain.done(dve.memset(vrow[:, :, :, VW - 1:VS], 1.0))
                chain.done(dve.memset(rows[:, :, :, :], 0.0))
                dve.wait_ge(s_const, 16 * 5)
                chain.link(dve.tensor_copy(code[:, :], code_f[:, :]))
                dve.sem_inc(s_init, 1)
                for l in range(2):
                    dve.wait_ge(s_wt, l + 1)
                    dve.tensor_copy(WT[:, :], ps[:, 0, 0:P]).then_inc(s_wts, 1)
                    dve.wait_ge(s_wa, l + 1)
                    qh = 1 - l
                    dve.tensor_copy(Wx[l][:, F:F + 1], ps[:, 1, qh:qh + 1]).then_inc(s_was, 1)
                    dve.tensor_copy(Wx[l][:, F + 1:F + 2], ps[:, 1, 1 - qh:2 - qh]).then_inc(s_was, 1)
                chain.restart()

            def layernorm(layer):
                with dve.Fori(0, NC2) as cc:
                    c = layer * NC2 + cc
                    for b in range(2):
                        xb = xin[:, b]
                        mean, var, std, rstd = (stat[:, i, :] for i in range(4))
                        dve.wait_ge(s_xin[b], 16 * (c + 1))
                        chain.link(dve.tensor_reduce(var, xb, AX.X, ALU.add))
                        chain.link(dve.tensor_scalar(mean, var, 1.0 / F, None, ALU.mult))
                        chain.link(dve.tensor_tensor(cen[:, :, :], xb, stat[:, 0, :, None].to_broadcast([P, CH, F]), ALU.subtract))
                        chain.link(dve.tensor_tensor(sq[:, :, :], cen[:, :, :], cen[:, :, :], ALU.mult))
                        chain.link(dve.tensor_reduce(var, sq[:, :, :], AX.X, ALU.add))
                        chain.link(dve.tensor_scalar(std, var, 1.0 / F, EPS, ALU.mult, ALU.add))
                        dve.sem_inc(s_var[b], 1)
                        dve.wait_ge(s_std[b], c + 1)
                        chain.link(dve.reciprocal(rstd, std))
                        dve.wait_ge(s_hT[b], c + 1)
                        dve.scalar_tensor_tensor(hrow[:, b], cen[:, :, :], 0.0, stat[:, 3, :, None].to_broadcast([P, CH, F]),
                                                 ALU.max, ALU.mult).then_inc(s_h[b], 1)
                    chain.restart()

            def value_sums(layer):
                dve.wait_ge(s_sum, layer + 1)
                dve.tensor_copy(sumrep[:, 0:VW], ps[:, 7, 0:VW]).then_inc(s_sumrep, 1)
                dve.wait_ge(s_sumrep, layer + 1)

            def decode(at_words, at_idx):
                chain.link(dve.tensor_copy(topi[:, :, :], top[:, :, :]))
                half = topi[:, :, :].bitcast(U16).rearrange("p w (s h) -> p w s h", h=2)
                chain.done(dve.tensor_copy(words[:, at_words].rearrange("p (s w) -> p w s", w=NW), half[:, :, :, 0]))
                chain.link(dve.tensor_scalar(blk[:, :], half[:, 0, :, 1], -1.0, 0.0, ALU.add, ALU.max))
                chain.link(dve.tensor_scalar(idx[:, at_idx], blk[:, :], float(P), lane[:, 0:1], ALU.mult, ALU.add))

            def pack():
                with dve.Fori(0, T2) as tt:
                    for b in range(2):
                        t = 2 * tt + b
                        for k in range(LD):
                            dve.wait_ge(s_adj[k], 16 * (t + 1))
                            dve.wait_ge(s_pack[k % 2], 2 * t + k // 2 + 1)
                            dve.tensor_scalar(a01[:, k % 2, :], adj_in[:, k, :], 0.0, None, ALU.is_gt).then_inc(s_conv[k], 1)
                        for h in range(2):
                            dve.wait_ge(s_pack[h], 2 * t + 3)
                        pk = ps[:, b, 0:T * NW]
                        chain.link(dve.tensor_reduce(occ[:, :], pk.rearrange("p (c w) -> p c w", w=NW), AX.X, ALU.max))
                        chain.done(dve.tensor_scalar(occ01[:, :], occ[:, :], 0.0, None, ALU.is_gt))
                        chain.link(dve.scalar_tensor_tensor(base[:, :], occ[:, :], 0.0, blockcode[:, :], ALU.is_gt, ALU.mult))
                        dve.tensor_reduce(cnt[:, b:b + 1], occ01[:, :], AX.X, ALU.add).then_inc(s_cnt[b], 1)
                        chain.link(dve.tensor_tensor(codes[:, :, :], pk.rearrange("p (c w) -> p w c", w=NW),
                                                     base[:, None, :].to_broadcast([P, NW, T]), ALU.add))
                        dve.sem_inc(s_code[b], 1)
                        for w in range(NW):
                            chain.done(dve.max(top[:, w, :], codes[:, w, :]))
                        chain.wait()
                        decode(bass.ds(t * T * NW, G * NW), bass.ds(t * T, G))
                        dve.wait_ge(s_cntT[b], tt + 1)
                        chain.link(dve.tensor_reduce(nmax[:, :], ps[0:1, 2 + b, 0:P], AX.X, ALU.max))
                        chain.link(dve.tensor_scalar(nslots[0:1, bass.ds(t, 1)], nmax[:, :], 1.0, None, ALU.max))
                        n = dve.value_load(nslots[0:1, bass.ds(t, 1)], min_val=1, max_val=T)
                        chain.restart()
                        if T > G:
                            with dve.If(n > G):
                                with dve.Fori(1, (n + G - 1) // G) as r:
                                    for w in range(NW):
                                        chain.done(dve.match_replace(codes[:, w, :], top[:, w, :], codes[:, w, :], 0.0))
                                    chain.wait()
                                    for w in range(NW):
                                        chain.done(dve.max(top[:, w, :], codes[:, w, :]))
                                    chain.wait()
                                    decode(bass.ds(t * T * NW + r * G * NW, G * NW), bass.ds(t * T + r * G, G))
                                    chain.restart()
                chain.link(dve.tensor_scalar(nlast[:, :], nslots[:, :], -1.0, None, ALU.add))
                chain.link(dve.tensor_scalar(nlast[:, :], nlast[:, :], G - 1, None, ALU.bitwise_and))
                chain.link(dve.tensor_scalar(nlast[:, :], nlast[:, :], 1.0, None, ALU.add))
                chain.restart()
                dve.sem_inc(s_packed, 1)

            def attend(layer):
                with dve.Fori(0, T2) as tt:
                    for b in range(2):
                        attend_tile(layer, tt, b)

            def attend_tile(layer, tt, b):
                t = 2 * tt + b
                nt = layer * T2 + tt
                kmax, z, lk, m, mnew, dm, corr = (col[:, b, i:i + 1] for i in range(7))
                q = qcol[:, bass.ds(t, 1)]
                scb = sc[:, b, :].rearrange("p (s i) -> p s i", s=G)
                dve.tensor_copy(qb[:, b, :], q.to_broadcast([P, P])).then_inc(s_qb[b], 1)
                chain.done(dve.memset(acc[:, b, :], 0.0))
                chain.done(dve.memset(m, FLOOR))
                chain.restart()
                n = dve.value_load(nslots[0:1, bass.ds(t, 1)], min_val=1, max_val=T)
                last = dve.value_load(nlast[0:1, bass.ds(t, 1)], min_val=1, max_val=G)
                with dve.Fori(0, (n + G - 1) // G) as g:
                    u = dve.snap(unit[b])
                    wd = words[:, bass.ds(t * T * NW + g * G * NW, G * NW)].rearrange("p (s w) -> p s w", w=NW)
                    chain.link(dve.tensor_tensor(
                        bits[:, :].rearrange("p (s w j) -> p (s w) j", s=G, w=NW),
                        words[:, bass.ds(t * T * NW + g * G * NW, G * NW)][:, :, None].to_broadcast([P, G * NW, WORD]),
                        bitmask[:, 0:WORD][:, None, :].to_broadcast([P, G * NW, WORD]), ALU.bitwise_and))
                    chain.link(dve.tensor_scalar(sc[:, b, :], bits[:, :], 0.0, MASKED, ALU.is_equal, ALU.mult))
                    with dve.If(n > (g + 1) * G):
                        dve.reg_add(gathered[b], gathered[b], G)
                    with dve.Else():
                        dve.reg_add(gathered[b], gathered[b], last)
                    dve.wait_ge(s_rows[b], dve.snap(gathered[b]) * 16)
                    chain.link(dve.tensor_tensor(scb, scb, rows[:, b, :, KC:KC + 1].to_broadcast([P, G, P]), ALU.add))
                    dve.tensor_reduce(kr[:, b, :], scb.rearrange("p s i -> p i s"), AX.X, ALU.max).then_inc(s_kr[b], 1)
                    dve.wait_ge(s_qrep[b], nt + 1)
                    dve.wait_ge(s_kr[b], u)
                    chain.link(dve.tensor_tensor(scb, scb, ps[:, 4 + b, 0:P][:, None, :].to_broadcast([P, G, P]), ALU.add))
                    chain.link(dve.scalar_tensor_tensor(scb, scb, ALPHA, scb, ALU.mult, ALU.max))
                    dve.wait_ge(s_kT[b], u)
                    chain.link(dve.tensor_reduce(kmax, ps[:, 2 + b, 0:P], AX.X, ALU.max))
                    chain.link(dve.tensor_tensor(z, kmax, q, ALU.add))
                    chain.link(dve.scalar_tensor_tensor(lk, z, ALPHA, z, ALU.mult, ALU.max))
                    chain.link(dve.tensor_tensor(mnew, lk, m, ALU.max))
                    dve.tensor_copy(mb[:, b, :], mnew.to_broadcast([P, P])).then_inc(s_mb[b], 1)
                    dve.tensor_tensor(dm, m, mnew, ALU.subtract).then_inc(s_dm[b], 1)
                    dve.wait_ge(s_dm[b], u)
                    chain.done(dve.tensor_copy(m, mnew))
                    dve.wait_ge(s_mrep[b], u)
                    dve.tensor_tensor(scb, scb, ps[:, 4 + b, P:2 * P][:, None, :].to_broadcast([P, G, P]),
                                      ALU.subtract).then_inc(s_d[b], 1)
                    dve.wait_ge(s_corr[b], u)
                    dve.wait_ge(s_pv[b], u + 1)
                    dve.scalar_tensor_tensor(acc[:, b, :], acc[:, b, :], corr, ps[:, 6 + b, 0:VW],
                                             ALU.mult, ALU.add).then_inc(s_acc[b], 1)
                    hold(dve, s_acc[b], u + 1)
                    chain.restart()
                    dve.reg_add(unit[b], unit[b], 1)
                empty, den, rec = (fcol[:, b, i:i + 1] for i in range(3))
                chain.link(dve.tensor_scalar(empty, acc[:, b, ONE:ONE + 1], 0.0, None, ALU.is_equal))
                chain.done(dve.scalar_tensor_tensor(num[:, b, :], sumrep[:, 0:F], empty, acc[:, b, 0:F], ALU.mult, ALU.add))
                chain.link(dve.scalar_tensor_tensor(den, empty, float(N), acc[:, b, ONE:ONE + 1], ALU.mult, ALU.add))
                chain.link(dve.reciprocal(rec, den))
                chain.link(dve.tensor_scalar(num[:, b, :], num[:, b, :], rec, None, ALU.mult))
                dve.tensor_scalar(hmin[:, b, :], num[:, b, :], 0.0, None, ALU.min).then_inc(s_hmin[b], 1)
                dve.wait_ge(s_em[b], nt + 1)
                chain.link(dve.scalar_tensor_tensor(num[:, b, :], num[:, b, :], 0.0, hmin[:, b, :], ALU.max, ALU.add))
                with dve.If(nt > 0):
                    hold(dve, s_out[b], 16 * nt)
                dve.wait_ge(s_xres[b], 16 * (nt + 1))
                dve.scalar_tensor_tensor(obuf[:, b, :], num[:, b, :], -1.0, xres[:, b, :], ALU.add, ALU.add).then_inc(s_fin[b], 1)
                chain.restart()

            credit(dve, *s_h, *s_conv, *s_code, *s_acc, *s_fin)
            init()
            layernorm(0)
            value_sums(0)
            pack()
            attend(0)
            layernorm(1)
            value_sums(1)
            attend(1)

        @block.tensor
        def _(pe):
            unit = [pe.alloc_register(f"pe_unit{b}") for b in range(2)]
            for b in range(2):
                pe.reg_mov(unit[b], 1)

            def weights():
                pe.wait_ge(s_const, 16 * 5)
                pe.wait_ge(s_memset, 1)
                pe.wait_ge(s_W, 16 * 4)
                for l in range(2):
                    if l:
                        pe.wait_ge(s_was, 2 * l)
                    pe.transpose(ps[:, 0, 0:P], Wx[l][:, 0:F], ident[:, :]).then_inc(s_wt, 1)
                    pe.wait_ge(s_wts, l + 1)
                    pe.matmul(ps[:, 1, 0:2], WT[:, :], acol[l][:, :], start=True, stop=True).then_inc(s_wa, 1)
                pe.wait_ge(s_was, 4)

            def project(layer):
                with pe.Fori(0, NC2) as cc:
                    c = layer * NC2 + cc
                    for b in range(2):
                        pe.wait_ge(s_h[b], c + 2)
                        pe.wait_ge(s_hTs[b], c + 1)
                        for q in range(CH):
                            ins = pe.transpose(ps[:, b, q * P:(q + 1) * P], hrow[:, b, q, :], ident[:, :])
                        ins.then_inc(s_hT[b], 1)
                        pe.wait_ge(s_hTs[b], c + 2)
                        pe.wait_ge(s_vrow[b], c + 1)
                        for q in range(CH):
                            ins = pe.matmul(ps[:, 2 + 2 * b + q // 2, (q % 2) * 256:(q % 2) * 256 + F + 2],
                                            hT[:, b, q * P:(q + 1) * P], Wx[layer][:, :], start=True, stop=True)
                        ins.then_inc(s_wh[b], 1)
                for b in range(2):
                    pe.wait_ge(s_vs[b], NC2 * (layer + 1) + 1)
                for q in range(CH):
                    ins = pe.matmul(ps[:, 7, 0:VW], ones[:, :], vsum[:, q, 0:VW], start=(q == 0), stop=(q == CH - 1))
                ins.then_inc(s_sum, 1)
                pe.wait_ge(s_sumrep, layer + 1)

            def pack():
                with pe.Fori(0, T2) as tt:
                    for b in range(2):
                        pe.wait_ge(s_code[b], tt + 1)
                        for k in range(LD):
                            pe.wait_ge(s_conv[k], 2 * tt + b + 2)
                            for c in range(LB):
                                at = (k * LB + c) * NW
                                ins = pe.matmul(ps[:, b, at:at + NW], a01[:, k % 2, c * P:(c + 1) * P], code[:, :],
                                                start=True, stop=True)
                            ins.then_inc(s_pack[k % 2], 1)
                        pe.wait_ge(s_cnt[b], tt + 1)
                        pe.transpose(ps[0:1, 2 + b, 0:P], cnt[:, b:b + 1], ident[:, :]).then_inc(s_cntT[b], 1)

            def attend(layer):
                with pe.Fori(0, T2) as tt:
                    nt = layer * T2 + tt
                    for b in range(2):
                        t = 2 * tt + b
                        pe.wait_ge(s_qb[b], nt + 1)
                        pe.matmul(ps[:, 4 + b, 0:P], qb[:, b, :], ident[:, :], start=True, stop=True).then_inc(s_qrep[b], 1)
                        n = pe.value_load(nslots[0:1, bass.ds(t, 1)], min_val=1, max_val=T)
                        with pe.Fori(0, (n + G - 1) // G) as g:
                            u = pe.snap(unit[b])
                            pe.wait_ge(s_kr[b], u)
                            pe.transpose(ps[:, 2 + b, 0:P], kr[:, b, :], ident[:, :]).then_inc(s_kT[b], 1)
                            pe.wait_ge(s_mb[b], u)
                            pe.matmul(ps[:, 4 + b, P:2 * P], mb[:, b, :], ident[:, :], start=True, stop=True).then_inc(s_mrep[b], 1)
                            pe.wait_ge(s_p[b], u)
                            pe.wait_ge(s_acc[b], u)
                            for s in range(G):
                                ins = pe.matmul(ps[:, 6 + b, 0:VW], pr[:, b, s * P:(s + 1) * P], rows[:, b, s, 0:VW],
                                                start=(s == 0), stop=(s == G - 1))
                            ins.then_inc(s_pv[b], 1)
                            pe.reg_add(unit[b], unit[b], 1)

            credit(pe, *s_hT, *s_pack, *s_pv)
            weights()
            project(0)
            pack()
            attend(0)
            project(1)
            attend(1)


def kernel(x, adj, L0_gnn_W, L0_gnn_a, L1_gnn_W, L1_gnn_a):
    import concourse.bacc as bacc
    from concourse.bass_utils import run_bass_kernel_spmd

    x, adj = np.ascontiguousarray(x), np.ascontiguousarray(adj)
    T = x.shape[0] // P
    i = np.arange(P)
    code = np.where(i[:, None] // WORD == np.arange(NW)[None, :], 2.0 ** (i[:, None] % WORD), 0.0).astype(np.float32)
    arrays = {
        "in_x": x, "in_adj": adj,
        "in_W0": np.ascontiguousarray(L0_gnn_W), "in_a0": np.ascontiguousarray(L0_gnn_a),
        "in_W1": np.ascontiguousarray(L1_gnn_W), "in_a1": np.ascontiguousarray(L1_gnn_a).reshape(-1),
        "c_ident": np.eye(P, dtype=np.float32),
        "c_code": code,
        "c_bitmask": np.broadcast_to((1 << (i % WORD)).astype(np.uint16), (P, P)).copy(),
        "c_block": np.broadcast_to(((np.arange(T) + 1) * BLOCK_CODE).astype(np.float32), (P, T)).copy(),
        "c_lane": i.astype(np.float32).reshape(P, 1),
    }
    nc = bacc.Bacc("TRN2", target_bir_lowering=False, num_devices=1)
    args = [nc.dram_tensor(k, a.shape, mybir.dt.from_np(a.dtype), kind="ExternalInput").ap() for k, a in arrays.items()]
    out = nc.dram_tensor("out_x", x.shape, F32, kind="ExternalOutput").ap()
    gat_two_layers(nc, *args, out)
    return run_bass_kernel_spmd(nc, [arrays], core_ids=[0]).results[0]["out_x"]
```

```python
from contextlib import ExitStack

import numpy as np
import concourse.bass as bass
from concourse import mybir
from concourse.alu_op_type import AluOpType as ALU

ACT = mybir.ActivationFunctionType
AX = mybir.AxisListType
F32 = mybir.dt.float32
BF16 = mybir.dt.bfloat16
I32 = mybir.dt.int32
U16 = mybir.dt.uint16

P = 128
WORD = 16
NW = P // WORD
FIND = 8
DEAL = 6
OPENING = ((1, 16), (2, 8), (3, 5), (2, 8), (4, 3), (4, 3))
Q, SLIM = 4, 2
CELLS = 16
RING = 4
CH = 4
EPS = 1e-5
ALPHA = 0.2
MASKED = -1e30
FLOOR = -1e28
BLOCK_CODE = 1 << WORD


CONSTANTS = 7


class Chain:

    def __init__(self, eng, sem):
        self.eng, self.sem, self.n = eng, sem, 0

    def done(self, ins):
        ins.then_inc(self.sem, 1)
        self.n += 1

    def wait(self):
        self.eng.wait_ge(self.sem, self.n)

    def link(self, ins):
        self.done(ins)
        self.wait()

    def restart(self):
        if self.n:
            self.wait()
            self.eng.sem_clear(self.sem)
            self.n = 0


def gat_two_layers(nc, x, adj, W0, a0, W1, a1, ident_c, code_c, bitmask_c, block_c, lane_c, iota_c, before_c, out):
    N, F = x.shape
    T = N // P
    T2 = T // 2
    NC2 = T // CH // 2
    LD = 4
    LW = N // LD
    LB = LW // P
    VW = F + 3
    QC, KC, ONE = F, F + 1, F + 2
    VS = VW + 1
    opening = [o for k, o in enumerate(OPENING) if sum(n for n, _ in OPENING[:k + 1]) <= T]
    first_alike = sum(n for n, _ in opening)
    NO = len(opening)
    NP = NO + (T - first_alike) // Q
    SL = max(-(-T // g) * g for g in [SLIM, DEAL] + [g for _, g in opening])
    PW = NW + 1
    NG = -(-T // SLIM)

    table = nc.dram_tensor("value_table", [N, VS], F32, kind="Internal").ap()
    x1 = nc.dram_tensor("x_between_layers", [N, F], F32, kind="Internal").ap()
    layer_in, layer_out = [x, x1], [x1, out]

    with ExitStack() as ctx:
        def sb(name, shape, dt=F32):
            return ctx.enter_context(nc.sbuf_tensor(name, shape, dt))

        def sem(name):
            return ctx.enter_context(nc.semaphore(name))

        def sem2(name):
            return [sem(f"{name}{i}") for i in range(2)]

        ident = sb("ident", [P, P])
        ones = sb("ones", [P, P])
        code_f = sb("code_f", [P, NW])
        code = sb("code", [P, NW], BF16)
        bitmask = sb("bitmask", [P, P], U16)
        blockcode = sb("blockcode", [P, T])
        lane = sb("lane", [P, 1])
        iota = sb("iota", [P, P])
        lanes_before = sb("lanes_before", [P, P])
        Wx = [sb(f"Wx{l}", [P, F + 2]) for l in range(2)]
        acol = [sb(f"acol{l}", [P, 2]) for l in range(2)]
        WT = sb("WT", [P, P])
        xin = sb("xin", [P, 2, CH, F])
        stat = sb("stat", [P, 4, CH])
        hrow = sb("hrow", [P, 2, CH, F])
        vrow = sb("vrow", [P, 2, CH, VS])
        vsum = sb("vsum", [P, CH, VS])
        qcol = sb("qcol", [P, T])
        sumrep = sb("sumrep", [P, VS])
        gathered = sb("gathered", [P, max(RING * CELLS * VS, LD * LW)])
        rows = gathered[:, 0:RING * CELLS * VS].rearrange("p (r c w) -> p r c w", r=RING, c=CELLS)
        adj_in = gathered[:, 0:LD * LW].bitcast(I32).rearrange("p (k n) -> p k n", k=LD)
        occ = sb("occ", [P, T])
        occ01 = sb("occ01", [P, T])
        base = sb("base", [P, T])
        cnt = sb("cnt", [P, 2])
        top = sb("top", [P, NW, FIND])
        topi = sb("topi", [P, NW, FIND], I32)
        rank = sb("rank", [P, 1])
        unused = sb("unused", [P, FIND])
        place = sb("place", [P, FIND], I32)
        to_lane = sb("to_lane", [P, FIND], I32)
        less_lane = sb("less_lane", [P, FIND])
        to_slot = sb("to_slot", [P, FIND], I32)
        at_slot = sb("at_slot", [P, FIND, DEAL])
        item = sb("item", [P, FIND, PW])
        items = sb("items", [P, FIND, DEAL, PW])
        dealt = sb("dealt", [P, SL, PW])
        total = sb("total", [1, 2], I32)
        nmax = sb("nmax", [1, 1])
        words = sb("words", [P, T, SL, NW], U16)
        idx = sb("idx", [P, T, SL], U16)
        nfind = sb("nfind", [1, T], I32)
        nslots = sb("nslots", [1, T], I32)
        npair = sb("npair", [1, NP], I32)
        ngather = sb("ngather", [1, NG, NP], I32)
        load = sb("load", [1, T], I32)
        idxs = sb("idxs", [P, RING, CELLS], I32)
        bits = sb("bits", [P, CELLS * P], U16)
        sc = sb("sc", [P, 2, CELLS * P])
        pr = sb("pr", [P, 2, CELLS * P])
        scratch = sc[:, :, :].rearrange("p b c -> p (b c)")
        lane_dist = scratch[:, 0:FIND * P].rearrange("p (s i) -> p s i", s=FIND)
        at_lane = scratch[:, FIND * P:2 * FIND * P].rearrange("p (s i) -> p s i", s=FIND)
        codes = scratch[:, 2 * FIND * P:2 * FIND * P + 2 * NW * T].rearrange("p (b w c) -> p b w c", b=2, w=NW)
        cen = scratch[:, 3 * FIND * P:3 * FIND * P + CH * F].rearrange("p (q f) -> p q f", q=CH)
        gsum = scratch[0:1, 3 * FIND * P:]
        a01 = pr[:, :, :].rearrange("p b c -> p (b c)")[:, 0:N // 2].bitcast(BF16).rearrange("p (k n) -> p k n", k=LD)
        hT = pr[:, :, 0:CH * P]
        kr = sb("kr", [P, 2, Q, P])
        qb = sb("qb", [P, 2, Q, P])
        mb = sb("mb", [P, 2, Q, P])
        found = sb("found", [P, 2, Q])
        m_run = sb("m_run", [P, 2, Q])
        m_new = sb("m_new", [P, 2, Q])
        m_fall = sb("m_fall", [P, 2, Q])
        corr = sb("corr", [P, 2, Q])
        acc = sb("acc", [P, 2, Q, VW])
        empty = sb("empty", [P, 2, Q])
        den = sb("den", [P, 2, Q])
        num = sb("num", [P, 2, Q, F])
        hmin = sb("hmin", [P, 2, Q, F])
        xres = sb("xres", [P, 2, Q, F])
        obuf = sb("obuf", [P, 2, Q, F])

        ps = ctx.enter_context(nc.psum_tensor("ps", [P, 8, 512], F32))

        kT = [ps[:, b, :].rearrange("p (t i) -> p t i", t=Q) for b in range(2)]
        mrep = kT
        qrep = [ps[:, 2 + b, :].rearrange("p (t i) -> p t i", t=Q) for b in range(2)]
        prod = [ps[:, 4 + 2 * b:6 + 2 * b, :].rearrange("p k (t w) -> p (k t) w", t=Q // 2)[:, :, 0:VW] for b in range(2)]

        s_const, s_memset, s_W, s_init = sem("s_const"), sem("s_memset"), sem("s_W"), sem("s_init")
        s_wt, s_wts, s_wa, s_was = sem("s_wt"), sem("s_wts"), sem("s_wa"), sem("s_was")
        s_var, s_std = sem2("s_var"), sem2("s_std")
        s_xin, s_h, s_hT, s_hTs = sem2("s_xin"), sem2("s_h"), sem2("s_hT"), sem2("s_hTs")
        s_wh, s_vrow, s_q, s_vs, s_tab = sem2("s_wh"), sem2("s_vrow"), sem2("s_q"), sem2("s_vs"), sem2("s_tab")
        s_sum, s_sumrep = sem("s_sum"), sem("s_sumrep")
        s_adj = [sem(f"s_adj{i}") for i in range(LD)]
        s_conv = [sem(f"s_conv{i}") for i in range(LD)]
        s_pack = [sem(f"s_pack{i}") for i in range(LD)]
        s_code, s_cnt, s_cntT = sem2("s_code"), sem2("s_cnt"), sem2("s_cntT")
        s_relu, s_place, s_dist, s_lane, s_items, s_dealt = sem("s_relu"), sem("s_place"), sem("s_dist"), sem("s_lane"), sem("s_items"), sem("s_dealt")
        s_slots, s_packed = sem("s_slots"), sem("s_packed")
        s_idx, s_rows, s_zq = [[sem(f"{n}{r}") for r in range(RING)] for n in ("s_idx", "s_rows", "s_zq")]
        s_kr, s_kT, s_mb, s_mrep = [[sem(f"{n}{r}") for r in range(RING)] for n in ("s_kr", "s_kT", "s_mb", "s_mrep")]
        s_d, s_p, s_pv, s_fall, s_corr = [[sem(f"{n}{r}") for r in range(RING)] for n in ("s_d", "s_p", "s_pv", "s_fall", "s_corr")]
        s_qb, s_qrep, s_hmin, s_em, s_fin = sem("s_qb"), sem("s_qrep"), sem("s_hmin"), sem("s_em"), sem("s_fin")
        s_xres, s_out = sem2("s_xres"), sem2("s_out")
        s_held = sem("s_held")
        s_vchain, s_gchain = sem("s_vchain"), sem("s_gchain")

        class Tiles:

            def __init__(self, p):
                if isinstance(p, int) and p < NO:
                    self.first, (self.n, self.G) = sum(n for n, _ in opening[:p]), opening[p]
                else:
                    self.first, self.n, self.G = p * Q - (NO * Q - first_alike), Q, SLIM

            def cells(self, flat):
                return flat[:, 0:self.n * self.G * P].rearrange("p (t s i) -> p t s i", t=self.n, s=self.G)

        def each_set(eng, body):
            p = 0
            while p < NP:
                rounds = (NP - 2 - p) // RING if p > NO else 0
                if rounds < 1:
                    body(p, Tiles(p), p % RING, p % 2)
                    p += 1
                    continue
                with eng.Fori(0, rounds) as j:
                    for i in range(p, p + RING):
                        body(j * RING + i, Tiles(j * RING + i), i % RING, i % 2)
                p += rounds * RING

        def half(p):
            return p // 2

        def registers(eng, name, start):
            regs = [eng.alloc_register(f"{name}{r}") for r in range(RING)]
            for r in regs:
                eng.reg_mov(r, start)
            return regs

        def chunk(dram, c):
            return dram[bass.ds(c * (CH * P), CH * P), :].rearrange("(q p) f -> p q f", p=P)

        def credit(eng, *sems):
            for s in sems:
                eng.sem_inc(s, 1)

        def hold(eng, s, value):
            eng.wait_ge(s, value)
            eng.sem_inc(s_held, 1)

        block = ctx.enter_context(nc.Block())

        @block.sync
        def _(sp):
            for dst, src in ((ident, ident_c), (code_f, code_c), (bitmask, bitmask_c), (blockcode, block_c),
                             (lane, lane_c), (iota, iota_c), (lanes_before, before_c)):
                sp.dma_start(dst[:, :], src).then_inc(s_const, 16)
            for l, (W, a) in enumerate(((W0, a0), (W1, a1))):
                sp.dma_start(Wx[l][:, 0:F], W).then_inc(s_W, 16)
                with nc.allow_non_contiguous_dma(reason="256 numbers"):
                    sp.dma_start(acol[l][:, :], a.rearrange("(s p) -> p s", p=P)).then_inc(s_W, 16)

            def load_x(layer):
                with sp.Fori(0, NC2) as cc:
                    for b in range(2):
                        sp.wait_ge(s_h[b], layer * NC2 + cc + 1)
                        sp.dma_start(xin[:, b], chunk(layer_in[layer], 2 * cc + b)).then_inc(s_xin[b], 16)
                        if b == 1:
                            store_values(layer, cc)

            def store_values(layer, cc):
                for b in range(2):
                    sp.wait_ge(s_vrow[b], layer * NC2 + cc + 2)
                    sp.dma_start(chunk(table, 2 * cc + b), vrow[:, b]).then_inc(s_tab[b], 16)

            def load_adj():
                with sp.Fori(0, T2) as tt:
                    for b in range(2):
                        t = 2 * tt + b
                        for k in range(LD):
                            sp.wait_ge(s_conv[k], t + 1)
                            sp.dma_start(adj_in[:, k], adj[bass.ds(t * P, P), k * LW:(k + 1) * LW]).then_inc(s_adj[k], 16)

            def rows_of(dram, S):
                return dram[bass.ds(S.first * P, S.n * P), :].rearrange("(t i) f -> i t f", t=S.n)

            def residual_and_store(layer):
                def store(p, b):
                    sp.wait_ge(s_fin, layer * NP + p + 3)
                    S = Tiles(p)
                    sp.dma_start(rows_of(layer_out[layer], S), obuf[:, b, 0:S.n]).then_inc(s_out[b], 16)

                def body(p, S, r, b):
                    sp.wait_ge(s_fin, layer * NP + p + 1)
                    sp.dma_start(xres[:, b, 0:S.n], rows_of(layer_in[layer], S)).then_inc(s_xres[b], 16)
                    if isinstance(p, int) and p == 0:
                        return
                    store(p - 1, 1 - b)

                each_set(sp, body)
                store(NP - 1, 1)
                for b in range(2):
                    sp.wait_ge(s_out[b], 16 * (NP // 2) * (layer + 1))

            load_x(0)
            load_adj()
            residual_and_store(0)
            load_x(1)
            residual_and_store(1)

        @block.gpsimd
        def _(pool):
            chain = Chain(pool, s_gchain)
            unit = registers(pool, "pool_unit", 1)

            def sum_values(layer):
                chain.link(pool.memset(vsum[:, :, :], 0.0))
                chain.restart()
                with pool.Fori(0, NC2) as cc:
                    for b in range(2):
                        pool.wait_ge(s_vrow[b], layer * NC2 + cc + 2)
                        ins = pool.tensor_tensor(vsum[:, :, 0:VW], vsum[:, :, 0:VW], vrow[:, b, :, 0:VW], ALU.add)
                        chain.link(ins)
                        pool.sem_inc(s_vs[b], 1)
                    chain.restart()

            def gather(layer):
                for b in range(2):
                    pool.wait_ge(s_tab[b], 16 * NC2 * (layer + 1))

                def gather_group(S, r, g):
                    u = pool.snap(unit[r])
                    hold(pool, s_pv[r], u)
                    c = S.n * S.G
                    pool.tensor_copy(idxs[:, r, 0:c].rearrange("p (t s) -> p t s", t=S.n),
                                     idx[:, bass.ds(S.first, S.n), bass.ds(g * S.G, S.G)]).then_inc(s_idx[r], 1)
                    n = [pool.value_load(nslots[0:1, bass.ds(S.first + i, 1)], min_val=1, max_val=T) for i in range(S.n)]
                    hold(pool, s_idx[r], u)
                    for i in range(S.n):
                        for s in range(S.G):
                            at = i * S.G + s
                            with pool.If(n[i] > g * S.G + s):
                                pool.indirect_dma_start(
                                    out=rows[:, r, at, :], out_offset=None, in_=table[:, :],
                                    in_offset=bass.IndirectOffsetOnAxis(ap=idxs[:, r, at:at + 1], axis=0),
                                ).then_inc(s_rows[r], 16)
                    pool.reg_add(unit[r], unit[r], 1)

                def body(p, S, r, b):
                    if isinstance(p, int) and p < RING:
                        pool.wait_ge(s_packed, p + 1)
                    n = pool.value_load(npair[0:1, bass.ds(p, 1)], min_val=1, max_val=T)
                    with pool.Fori(0, (n + S.G - 1) // S.G) as g:
                        gather_group(S, r, g)

                each_set(pool, body)

            credit(pool, *s_vs)
            pool.memset(words[:, :, :, :], 2 ** WORD - 1).then_inc(s_slots, 1)
            pool.memset(idx[:, :, :], 0).then_inc(s_slots, 1)
            pool.wait_ge(s_init, 1)
            sum_values(0)
            pool.wait_ge(s_packed, 1)
            gather(0)
            sum_values(1)
            gather(1)

        @block.scalar
        def _(act):
            unit = registers(act, "act_unit", 1)
            landed = registers(act, "act_landed", 0)

            def project(layer):
                with act.Fori(0, NC2) as cc:
                    c = layer * NC2 + cc
                    for b in range(2):
                        act.wait_ge(s_var[b], c + 1)
                        act.activation(stat[:, 2, :], stat[:, 2, :], ACT.Sqrt).then_inc(s_std[b], 1)
                        act.wait_ge(s_hT[b], c + 2)
                        act.activation(hT[:, b, :], ps[:, b, :], ACT.Copy).then_inc(s_hTs[b], 1)
                        with act.If(c > 0):
                            hold(act, s_tab[b], 16 * c)
                        act.wait_ge(s_wh[b], c + 1)
                        act.wait_ge(s_vs[b], c + 1)
                        act.wait_ge(s_q[b], c + 1)
                        wh = ps[:, 2 + 2 * b:4 + 2 * b, :].rearrange("p k (h w) -> p (k h) w", h=2)
                        act.activation(vrow[:, b, :, 0:F + 2], wh[:, :, 0:F + 2], ACT.Copy).then_inc(s_vrow[b], 1)
                        act.wait_ge(s_vrow[b], c + 2)
                        act.activation(qcol[:, bass.ds((2 * cc + b) * CH, CH)], vrow[:, b, :, QC], ACT.Copy).then_inc(s_q[b], 1)

            def attend(layer):
                def score(p, S, r, b, g):
                    more = act.value_load(ngather[0:1, bass.ds(g, 1), bass.ds(p, 1)], min_val=0, max_val=16 * S.n * S.G)
                    act.reg_add(landed[r], landed[r], more)
                    act.wait_ge(s_rows[r], act.snap(landed[r]))
                    for i in range(S.n):
                        for s in range(S.G):
                            ins = act.activation(S.cells(sc[:, b])[:, i, s, :], qrep[b][:, i, :], ACT.Identity,
                                                 bias=rows[:, r, i * S.G + s, KC:KC + 1])
                    ins.then_inc(s_zq[r], 1)

                def spread_query(S, b):
                    act.activation(qb[:, b, 0:S.n], qcol[:, bass.ds(S.first, S.n)][:, :, None].to_broadcast([P, S.n, P]),
                                   ACT.Copy).then_inc(s_qb, 1)

                def exponential(S, r, b):
                    act.activation(pr[:, b, 0:S.n * S.G * P], sc[:, b, 0:S.n * S.G * P], ACT.Exp).then_inc(s_p[r], 1)

                def exponentials(S, r, b):
                    u = act.snap(unit[r])
                    act.wait_ge(s_d[r], u)
                    exponential(S, r, b)
                    act.sem_inc(s_corr[r], 1)
                    act.reg_add(unit[r], unit[r], 1)

                def later_groups(p, S, r, b, n):
                    with act.Fori(1, (n + S.G - 1) // S.G) as g:
                        score(p, S, r, b, g)
                        u = act.snap(unit[r])
                        act.wait_ge(s_fall[r], u)
                        act.activation(corr[:, b, 0:S.n], m_fall[:, b, 0:S.n], ACT.Exp).then_inc(s_corr[r], 1)
                        act.wait_ge(s_d[r], u)
                        act.wait_ge(s_pv[r], u)
                        exponential(S, r, b)
                        act.reg_add(unit[r], unit[r], 1)

                def first_score(p, S, r, b):
                    act.wait_ge(s_qrep, layer * NP + p + 1)
                    score(p, S, r, b, 0)
                    if not (isinstance(p, int) and p == NP - 1):
                        spread_query(Tiles(p + 1), 1 - b)

                def elu_exponential(p, S, b):
                    act.wait_ge(s_hmin, layer * NP + p + 1)
                    act.activation(hmin[:, b, 0:S.n], hmin[:, b, 0:S.n], ACT.Exp).then_inc(s_em, 1)

                def body(p, S, r, b):
                    if isinstance(p, int) and p == 0:
                        spread_query(S, 0)
                        first_score(p, S, r, b)
                        return
                    r1, b1, S1 = (r - 1) % RING, 1 - b, Tiles(p - 1)
                    if T <= S1.G:
                        first_score(p, S, r, b)
                        exponentials(S1, r1, b1)
                        elu_exponential(p - 1, S1, b1)
                        return
                    n = act.value_load(npair[0:1, bass.ds(p - 1, 1)], min_val=1, max_val=T)
                    with act.If(n > S1.G):
                        exponentials(S1, r1, b1)
                        later_groups(p - 1, S1, r1, b1, n)
                        first_score(p, S, r, b)
                    with act.Else():
                        first_score(p, S, r, b)
                        exponentials(S1, r1, b1)
                    elu_exponential(p - 1, S1, b1)

                each_set(act, body)
                r, b, S = (NP - 1) % RING, (NP - 1) % 2, Tiles(NP - 1)
                exponentials(S, r, b)
                if T > S.G:
                    n = act.value_load(npair[0:1, NP - 1:NP], min_val=1, max_val=T)
                    with act.If(n > S.G):
                        later_groups(NP - 1, S, r, b, n)
                elu_exponential(NP - 1, S, b)

            def pack():
                turn = act.alloc_register("act_turn")
                act.reg_mov(turn, 1)

                def lanes():
                    u = act.snap(turn)
                    act.wait_ge(s_place, u)
                    for s in range(FIND):
                        ins = act.activation(lane_dist[:, s, :], iota[:, :], ACT.Abs, bias=less_lane[:, s:s + 1])
                    ins.then_inc(s_dist, 1)
                    act.wait_ge(s_dist, u)
                    act.activation(at_lane[:, :, :], lane_dist[:, :, :], ACT.Relu, bias=1.0, scale=-1.0).then_inc(s_lane, 1)
                    act.reg_add(turn, turn, 1)

                def convert(t):
                    act.wait_ge(s_adj[1], 16 * (t + 1))
                    act.wait_ge(s_pack[1], t + 1)
                    act.activation(a01[:, 1, :], adj_in[:, 1, :], ACT.Relu).then_inc(s_relu, 1)
                    act.wait_ge(s_relu, t + 1)
                    act.activation(a01[:, 1, :], a01[:, 1, :], ACT.Sign).then_inc(s_conv[1], 1)

                def further_lanes(t):
                    if T > FIND:
                        n = act.value_load(nfind[0:1, bass.ds(t, 1)], min_val=1, max_val=T)
                        with act.If(n > FIND):
                            with act.Fori(1, (n + FIND - 1) // FIND):
                                lanes()

                convert(0)
                convert(1)
                lanes()
                with act.Fori(2, T) as t:
                    convert(t)
                    further_lanes(t - 2)
                    lanes()
                further_lanes(T - 2)
                lanes()
                further_lanes(T - 1)

            credit(act, *s_hTs, *s_vrow, *s_q)
            project(0)
            pack()
            act.wait_ge(s_packed, 1)
            attend(0)
            project(1)
            attend(1)


        @block.vector
        def _(dve):
            chain = Chain(dve, s_vchain)
            unit = registers(dve, "dve_unit", 1)

            def init():
                dve.memset(ones[:, :], 1.0).then_inc(s_memset, 1)
                chain.done(dve.memset(vrow[:, :, :, VW - 1:VS], 1.0))
                chain.done(dve.memset(acc[:, :, :, :], 0.0))
                dve.wait_ge(s_const, 16 * CONSTANTS)
                chain.link(dve.tensor_copy(code[:, :], code_f[:, :]))
                dve.sem_inc(s_init, 1)
                for l in range(2):
                    dve.wait_ge(s_wt, l + 1)
                    dve.tensor_copy(WT[:, :], ps[:, 0, 0:P]).then_inc(s_wts, 1)
                    dve.wait_ge(s_wa, l + 1)
                    qh = 1 - l
                    dve.tensor_copy(Wx[l][:, F:F + 1], ps[:, 1, qh:qh + 1]).then_inc(s_was, 1)
                    dve.tensor_copy(Wx[l][:, F + 1:F + 2], ps[:, 1, 1 - qh:2 - qh]).then_inc(s_was, 1)
                chain.restart()

            def layernorm(layer):
                with dve.Fori(0, NC2) as cc:
                    c = layer * NC2 + cc
                    for b in range(2):
                        xb = xin[:, b]
                        mean, var, std, rstd = (stat[:, i, :] for i in range(4))
                        dve.wait_ge(s_xin[b], 16 * (c + 1))
                        chain.link(dve.tensor_reduce(var, xb, AX.X, ALU.add))
                        chain.link(dve.tensor_scalar(mean, var, 1.0 / F, None, ALU.mult))
                        chain.link(dve.tensor_tensor(cen, xb, stat[:, 0, :, None].to_broadcast([P, CH, F]), ALU.subtract))
                        dve.wait_ge(s_hT[b], c + 1)
                        chain.link(dve.tensor_tensor(hrow[:, b], cen, cen, ALU.mult))
                        chain.link(dve.tensor_reduce(var, hrow[:, b], AX.X, ALU.add))
                        chain.link(dve.tensor_scalar(std, var, 1.0 / F, EPS, ALU.mult, ALU.add))
                        dve.sem_inc(s_var[b], 1)
                        dve.wait_ge(s_std[b], c + 1)
                        chain.link(dve.reciprocal(rstd, std))
                        dve.scalar_tensor_tensor(hrow[:, b], cen, 0.0, stat[:, 3, :, None].to_broadcast([P, CH, F]),
                                                 ALU.max, ALU.mult).then_inc(s_h[b], 1)
                    chain.restart()

            def value_sums(layer):
                dve.wait_ge(s_sum, layer + 1)
                dve.tensor_copy(sumrep[:, 0:VW], ps[:, 7, 0:VW]).then_inc(s_sumrep, 1)
                dve.wait_ge(s_sumrep, layer + 1)

            deal = registers(dve, "dve_deal", 1)[0]

            def places(b):
                chain.link(dve.tensor_scalar(unused[:, :], iota[:, 0:FIND], cnt[:, b:b + 1], float(T * P), ALU.is_ge, ALU.mult))
                chain.link(dve.scalar_tensor_tensor(place[:, :], iota[:, 0:FIND], rank[:, 0:1], unused[:, :], ALU.add, ALU.add))
                chain.done(dve.tensor_scalar(to_lane[:, :], place[:, :], P - 1, None, ALU.bitwise_and))
                chain.done(dve.tensor_scalar(to_slot[:, :], place[:, :], P.bit_length() - 1, None, ALU.logical_shift_right))
                chain.wait()
                chain.link(dve.tensor_scalar(less_lane[:, :], to_lane[:, :], -1.0, None, ALU.mult))
                dve.sem_inc(s_place, 1)

            def find(b):
                for w in range(NW):
                    chain.done(dve.max(top[:, w, :], codes[:, b, w, :]))
                chain.wait()
                chain.link(dve.tensor_copy(topi[:, :, :], top[:, :, :]))
                parts = topi[:, :, :].bitcast(U16).rearrange("p w (s h) -> p s w h", h=2)
                chain.done(dve.tensor_copy(item[:, :, 0:NW], parts[:, :, :, 0]))
                chain.done(dve.tensor_scalar(item[:, :, NW], parts[:, :, 0, 1], float(P), lane[:, 0:1], ALU.mult, ALU.add))

            def send_items():
                chain.link(dve.tensor_tensor(at_slot[:, :, :], to_slot[:, :, None].to_broadcast([P, FIND, DEAL]),
                                             iota[:, None, 0:DEAL].to_broadcast([P, FIND, DEAL]), ALU.is_equal))
                dve.tensor_tensor(items[:, :, :, :], item[:, :, None, :].to_broadcast([P, FIND, DEAL, PW]),
                                  at_slot[:, :, :, None].to_broadcast([P, FIND, DEAL, PW]), ALU.mult).then_inc(s_items, 1)

            def take_dealt():
                dve.wait_ge(s_dealt, dve.snap(deal))
                dve.reg_add(deal, deal, 1)

            def dealt_at(e):
                return dealt[:, bass.ds(e * DEAL, DEAL), :]

            dealt_ps = ps[:, 4, 0:DEAL * PW].rearrange("p (s w) -> p s w", s=DEAL)

            def keep_dealt(t, e):
                chain.done(dve.tensor_scalar(words[:, bass.ds(t, 1), bass.ds(e * DEAL, DEAL), :].rearrange("p t s w -> p (t s) w"),
                                             dealt_at(e)[:, :, 0:NW], -1.0, float(2 ** WORD - 1), ALU.mult, ALU.add))
                chain.done(dve.tensor_copy(idx[:, bass.ds(t, 1), bass.ds(e * DEAL, DEAL)].rearrange("p t s -> p (t s)"),
                                           dealt_at(e)[:, :, NW]))

            def next_deal():
                chain.link(dve.tensor_scalar(to_slot[:, :], to_slot[:, :], -float(DEAL), None, ALU.add))

            def further_deals(t, b):
                n = dve.value_load(load[0:1, bass.ds(t, 1)], min_val=0, max_val=2 * T)
                chain.restart()
                with dve.If(n > FIND):
                    rounds = (dve.value_load(nfind[0:1, bass.ds(t, 1)], min_val=1, max_val=T) + FIND - 1) // FIND
                    deals = (dve.value_load(nslots[0:1, bass.ds(t, 1)], min_val=1, max_val=T) + DEAL - 1) // DEAL
                    with dve.If(deals > 1):
                        with dve.Fori(1, deals) as e:
                            next_deal()
                            send_items()
                            take_dealt()
                            chain.link(dve.tensor_copy(dealt_at(e), dealt_ps))
                            chain.restart()
                    if T > FIND:
                        with dve.If(rounds > 1):
                            with dve.Fori(1, rounds):
                                for w in range(NW):
                                    chain.done(dve.match_replace(codes[:, b, w, :], top[:, w, :], codes[:, b, w, :], 0.0))
                                chain.done(dve.tensor_scalar(cnt[:, b:b + 1], cnt[:, b:b + 1], -float(FIND), None, ALU.add))
                                chain.done(dve.tensor_scalar(rank[:, :], rank[:, :], float(FIND), None, ALU.add))
                                chain.wait()
                                places(b)
                                find(b)
                                chain.restart()
                                with dve.Fori(0, deals) as e:
                                    send_items()
                                    take_dealt()
                                    chain.done(dve.tensor_tensor(dealt_at(e), dealt_at(e), dealt_ps, ALU.add))
                                    next_deal()
                                    chain.restart()
                    with dve.If(deals > 1):
                        with dve.Fori(1, deals) as e:
                            keep_dealt(t, e)
                            chain.restart()

            def pack():
                def convert(t, k):
                    dve.wait_ge(s_adj[k], 16 * (t + 1))
                    dve.wait_ge(s_pack[k], t + 1)
                    dve.tensor_scalar(a01[:, k, :], adj_in[:, k, :], 0.0, None, ALU.is_gt).then_inc(s_conv[k], 1)

                def count_slots(t, b):
                    pc = ps[:, 2 + b, :]
                    dve.wait_ge(s_cntT[b], half(t) + 1)
                    chain.done(dve.tensor_reduce(nmax[:, :], pc[0:1, 0:P], AX.X, ALU.max))
                    chain.done(dve.tensor_scalar(total[:, 0:1], pc[0:1, P + 1:P + 2], float(P - 1), None, ALU.add))
                    chain.done(dve.tensor_copy(rank[:, :], pc[:, P:P + 1]))
                    chain.wait()
                    chain.done(dve.tensor_scalar(nfind[0:1, bass.ds(t, 1)], nmax[:, :], 1.0, None, ALU.max))
                    chain.link(dve.tensor_scalar(total[:, 1:2], total[:, 0:1], P.bit_length() - 1, None, ALU.logical_shift_right))
                    chain.link(dve.tensor_scalar(nslots[0:1, bass.ds(t, 1)], total[:, 1:2], 1.0, None, ALU.max))
                    chain.done(dve.scalar_tensor_tensor(load[0:1, bass.ds(t, 1)], total[:, 1:2], float(FIND - DEAL), nmax[:, :],
                                                        ALU.add, ALU.max))

                def keep_slots(t, b):
                    take_dealt()
                    chain.link(dve.tensor_copy(dealt_at(0), dealt_ps))
                    if T > min(FIND, DEAL):
                        further_deals(t, b)
                    keep_dealt(t, 0)

                def body(t, b, before, after):
                    pk = ps[:, 1 - b, 0:T * NW]
                    if after:
                        convert(t, 0)
                    if before:
                        for k in range(LD):
                            dve.wait_ge(s_pack[k], t + 1)
                        chain.done(dve.tensor_reduce(occ[:, :], pk.rearrange("p (c w) -> p c w", w=NW), AX.X, ALU.max))
                    if before:
                        chain.wait()
                        chain.done(dve.scalar_tensor_tensor(base[:, :], occ[:, :], 0.0, blockcode[:, :], ALU.is_gt, ALU.mult))
                        chain.link(dve.tensor_scalar(occ01[:, :], occ[:, :], 0.0, None, ALU.is_gt))
                        dve.tensor_reduce(cnt[:, 1 - b:2 - b], occ01[:, :], AX.X, ALU.add).then_inc(s_cnt[1 - b], 1)
                        dve.tensor_tensor(codes[:, 1 - b], pk.rearrange("p (c w) -> p w c", w=NW),
                                          base[:, None, :].to_broadcast([P, NW, T]), ALU.add).then_inc(s_code[1 - b], 1)
                    if after:
                        convert(t, 2)
                    if before:
                        hold(dve, s_code[1 - b], half(t - 1) + 2)
                        if not (isinstance(t, int) and t == 1):
                            keep_slots(t - 2, b)
                        count_slots(t - 1, 1 - b)
                        places(1 - b)
                        find(1 - b)
                        chain.wait()
                        send_items()
                    if after:
                        convert(t, 3)
                    chain.restart()

                body(0, 0, False, True)
                body(1, 1, True, True)
                with dve.Fori(0, T2 - 1) as j:
                    for i in (2, 3):
                        body(2 * j + i, i % 2, True, True)
                body(T, 0, True, False)
                keep_slots(T - 1, 1)

                alike = [(first_alike, T, NO, Q, SLIM)] if NP > NO else []
                for t0, t1, p0, n, G in [(Tiles(p).first, Tiles(p).first + Tiles(p).n, p, Tiles(p).n, Tiles(p).G)
                                         for p in range(NO)] + alike:
                    groups, sets = -(-T // G), (t1 - t0) // n
                    chain.done(dve.tensor_reduce(npair[:, p0:p0 + sets], nslots[:, t0:t1].rearrange("o (p i) -> o p i", i=n),
                                                 AX.X, ALU.max))
                    clip = scratch[0:1, 0:groups * (t1 - t0)].rearrange("o (g t) -> o g t", g=groups)
                    chain.link(dve.scalar_tensor_tensor(clip, iota[0:1, 0:groups, None].to_broadcast([1, groups, t1 - t0]), -float(G),
                                                        nslots[:, None, t0:t1].to_broadcast([1, groups, t1 - t0]), ALU.mult, ALU.add))
                    chain.link(dve.tensor_scalar(clip, clip, 0.0, float(G), ALU.max, ALU.min))
                    count = gsum[:, 0:groups * sets].rearrange("o (g p) -> o g p", g=groups)
                    chain.link(dve.tensor_reduce(count, clip.rearrange("o g (p i) -> o g p i", i=n), AX.X, ALU.add))
                    chain.link(dve.tensor_scalar(ngather[:, 0:groups, p0:p0 + sets], count, 16.0, None, ALU.mult))
                for r in range(RING):
                    chain.link(dve.memset(rows[:, r], 0.0))
                    dve.sem_inc(s_packed, 1)
                chain.restart()

            def attend(layer):
                def mask_and_max(p, S, r, b, g):
                    u = dve.snap(unit[r])
                    c = S.n * S.G
                    wd = words[:, bass.ds(S.first, S.n), bass.ds(g * S.G, S.G), :].rearrange("p t s w -> p t (s w)")
                    chain.link(dve.tensor_tensor(
                        bits[:, 0:c * P].rearrange("p (t x j) -> p t x j", t=S.n, j=WORD),
                        wd[:, :, :, None].to_broadcast([P, S.n, S.G * NW, WORD]),
                        bitmask[:, None, None, 0:WORD].to_broadcast([P, S.n, S.G * NW, WORD]), ALU.bitwise_and))
                    dve.wait_ge(s_zq[r], u)
                    x = sc[:, b, 0:c * P]
                    chain.link(dve.scalar_tensor_tensor(x, bits[:, 0:c * P], MASKED, x, ALU.mult, ALU.add))
                    chain.link(dve.scalar_tensor_tensor(x, x, ALPHA, x, ALU.mult, ALU.max))
                    dve.tensor_reduce(kr[:, b, 0:S.n], S.cells(sc[:, b]).rearrange("p t s i -> p t i s"), AX.X, ALU.max).then_inc(s_kr[r], 1)

                def row_max(S, r, b, first):
                    u = dve.snap(unit[r])
                    run, new = m_run[:, b, 0:S.n], m_new[:, b, 0:S.n]
                    dve.wait_ge(s_kT[r], u)
                    chain.link(dve.tensor_reduce(found[:, b, 0:S.n], kT[b][:, 0:S.n], AX.X, ALU.max))
                    if first:
                        dve.memset(corr[:, b], 0.0).then_inc(s_fall[r], 1)
                        chain.link(dve.tensor_scalar(run, found[:, b, 0:S.n], FLOOR, None, ALU.max))
                    else:
                        chain.link(dve.tensor_tensor(new, found[:, b, 0:S.n], run, ALU.max))
                        dve.tensor_tensor(m_fall[:, b, 0:S.n], run, new, ALU.subtract).then_inc(s_fall[r], 1)
                        dve.wait_ge(s_fall[r], u)
                        chain.link(dve.tensor_copy(run, new))
                    dve.tensor_copy(mb[:, b, 0:S.n], run[:, :, None].to_broadcast([P, S.n, P])).then_inc(s_mb[r], 1)

                def less_max(S, r, b, later=False):
                    u = dve.snap(unit[r])
                    if later:
                        dve.wait_ge(s_corr[r], u)
                    dve.wait_ge(s_fall[r], u)
                    dve.wait_ge(s_mrep[r], u)
                    x = S.cells(sc[:, b])
                    dve.tensor_tensor(x, x, mrep[b][:, 0:S.n, None, :].to_broadcast([P, S.n, S.G, P]), ALU.subtract).then_inc(s_d[r], 1)
                    dve.reg_add(unit[r], unit[r], 1)

                def accumulate(S, r, b):
                    dve.wait_ge(s_pv[r], dve.snap(unit[r]))
                    for i in range(S.n):
                        chain.done(dve.scalar_tensor_tensor(acc[:, b, i, :], acc[:, b, i, :], corr[:, b, i:i + 1],
                                                            prod[b][:, i, :], ALU.mult, ALU.add))
                    chain.wait()

                def normalise(S, r, b):
                    accumulate(S, r, b)
                    total, miss, over, x = acc[:, b, 0:S.n, ONE], empty[:, b, 0:S.n], den[:, b, 0:S.n], num[:, b, 0:S.n]
                    chain.link(dve.tensor_scalar(miss, total, 0.0, None, ALU.is_equal))
                    chain.done(dve.scalar_tensor_tensor(over, miss, float(N), total, ALU.mult, ALU.add))
                    for i in range(S.n):
                        chain.done(dve.scalar_tensor_tensor(x[:, i, :], sumrep[:, 0:F], empty[:, b, i:i + 1],
                                                            acc[:, b, i, 0:F], ALU.mult, ALU.add))
                    chain.wait()
                    chain.link(dve.reciprocal(over, over))
                    for i in range(S.n):
                        chain.done(dve.tensor_scalar(x[:, i, :], x[:, i, :], den[:, b, i:i + 1], None, ALU.mult))
                    chain.wait()
                    dve.tensor_scalar(hmin[:, b, 0:S.n], x, 0.0, None, ALU.min).then_inc(s_hmin, 1)

                def add_residual(p, S, b):
                    x = num[:, b, 0:S.n]
                    dve.wait_ge(s_em, layer * NP + p + 1)
                    chain.link(dve.scalar_tensor_tensor(x, x, 0.0, hmin[:, b, 0:S.n], ALU.max, ALU.add))
                    dve.wait_ge(s_xres[b], 16 * (layer * (NP // 2) + half(p) + 1))
                    if layer or not isinstance(p, int) or p > 1:
                        dve.wait_ge(s_out[b], 16 * (layer * (NP // 2) + half(p)))
                    dve.scalar_tensor_tensor(obuf[:, b, 0:S.n], x, -1.0, xres[:, b, 0:S.n], ALU.add, ALU.add).then_inc(s_fin, 1)

                def body(p, S, r, b):
                    r1, b1, later = (r - 1) % RING, 1 - b, not (isinstance(p, int) and p == 0)
                    S1 = Tiles(p - 1) if later else None
                    mask_and_max(p, S, r, b, 0)
                    if later:
                        normalise(S1, r1, b1)
                    row_max(S, r, b, True)
                    if later:
                        add_residual(p - 1, S1, b1)
                    less_max(S, r, b)
                    n = dve.value_load(npair[0:1, bass.ds(p, 1)], min_val=1, max_val=T)
                    chain.restart()
                    if T > S.G:
                        with dve.If(n > S.G):
                            with dve.Fori(1, (n + S.G - 1) // S.G) as g:
                                accumulate(S, r, b)
                                mask_and_max(p, S, r, b, g)
                                row_max(S, r, b, False)
                                less_max(S, r, b, True)
                                chain.restart()

                each_set(dve, body)
                S = Tiles(NP - 1)
                normalise(S, (NP - 1) % RING, (NP - 1) % 2)
                add_residual(NP - 1, S, (NP - 1) % 2)
                chain.restart()

            credit(dve, *s_h, *s_conv, *s_code, s_fin, s_fin)
            init()
            layernorm(0)
            value_sums(0)
            dve.wait_ge(s_slots, 2)
            pack()
            attend(0)
            layernorm(1)
            value_sums(1)
            attend(1)

        @block.tensor
        def _(pe):
            unit = registers(pe, "pe_unit", 1)
            deal, turn = registers(pe, "pe_deal", 1)[0:2]

            def weights():
                pe.wait_ge(s_const, 16 * CONSTANTS)
                pe.wait_ge(s_memset, 1)
                pe.wait_ge(s_W, 16 * 4)
                for l in range(2):
                    if l:
                        pe.wait_ge(s_was, 2 * l)
                    pe.transpose(ps[:, 0, 0:P], Wx[l][:, 0:F], ident[:, :]).then_inc(s_wt, 1)
                    pe.wait_ge(s_wts, l + 1)
                    pe.matmul(ps[:, 1, 0:2], WT[:, :], acol[l][:, :], start=True, stop=True).then_inc(s_wa, 1)
                pe.wait_ge(s_was, 4)

            def project(layer):
                with pe.Fori(0, NC2) as cc:
                    c = layer * NC2 + cc
                    for b in range(2):
                        pe.wait_ge(s_h[b], c + 2)
                        pe.wait_ge(s_hTs[b], c + 1)
                        for q in range(CH):
                            ins = pe.transpose(ps[:, b, q * P:(q + 1) * P], hrow[:, b, q, :], ident[:, :])
                        ins.then_inc(s_hT[b], 1)
                        pe.wait_ge(s_hTs[b], c + 2)
                        pe.wait_ge(s_vrow[b], c + 1)
                        for q in range(CH):
                            ins = pe.matmul(ps[:, 2 + 2 * b + q // 2, (q % 2) * 256:(q % 2) * 256 + F + 2],
                                            hT[:, b, q * P:(q + 1) * P], Wx[layer][:, :], start=True, stop=True)
                        ins.then_inc(s_wh[b], 1)
                for b in range(2):
                    pe.wait_ge(s_vs[b], NC2 * (layer + 1) + 1)
                for q in range(CH):
                    ins = pe.matmul(ps[:, 7, 0:VW], ones[:, :], vsum[:, q, 0:VW], start=(q == 0), stop=(q == CH - 1))
                ins.then_inc(s_sum, 1)
                pe.wait_ge(s_sumrep, layer + 1)

            def pack():
                def words_of(t, b):
                    third = not isinstance(t, int) or t > 1
                    if third:
                        deal_out()
                    pe.wait_ge(s_code[b], half(t) + 1)
                    for k in range(LD):
                        pe.wait_ge(s_conv[k], t + 2)
                        for c in range(LB):
                            at = (k * LB + c) * NW
                            ins = pe.matmul(ps[:, b, at:at + NW], a01[:, k, c * P:(c + 1) * P], code[:, :],
                                            start=True, stop=True)
                        ins.then_inc(s_pack[k], 1)
                        if k == 0 and (third or t == 1):
                            counts_of(t - 1, 1 - b)
                        if k == 0 and third:
                            further_deals(t - 2)

                def counts_of(t, b):
                    pe.wait_ge(s_cnt[b], half(t) + 1)
                    n = cnt[:, b:b + 1]
                    pe.transpose(ps[0:1, 2 + b, 0:P], n, ident[:, :])
                    pe.matmul(ps[:, 2 + b, P:P + 1], lanes_before[:, :], n, start=True, stop=True)
                    pe.matmul(ps[0:1, 2 + b, P + 1:P + 2], n, ones[:, 0:1], start=True, stop=True).then_inc(s_cntT[b], 1)

                def deal_out():
                    d, u = pe.snap(deal), pe.snap(turn)
                    pe.wait_ge(s_items, d)
                    pe.wait_ge(s_lane, u)
                    for s in range(FIND):
                        ins = pe.matmul(ps[:, 4, 0:DEAL * PW], at_lane[:, s, :], items[:, s].rearrange("p d w -> p (d w)"),
                                        start=(s == 0), stop=(s == FIND - 1))
                    ins.then_inc(s_dealt, 1)
                    pe.reg_add(deal, deal, 1)

                def further_deals(t):
                    if T <= min(FIND, DEAL):
                        pe.reg_add(turn, turn, 1)
                        return
                    n = pe.value_load(load[0:1, bass.ds(t, 1)], min_val=0, max_val=2 * T)
                    with pe.If(n > FIND):
                        rounds = (pe.value_load(nfind[0:1, bass.ds(t, 1)], min_val=1, max_val=T) + FIND - 1) // FIND
                        deals = (pe.value_load(nslots[0:1, bass.ds(t, 1)], min_val=1, max_val=T) + DEAL - 1) // DEAL
                        with pe.If(deals > 1):
                            with pe.Fori(1, deals):
                                deal_out()
                        pe.reg_add(turn, turn, 1)
                        if T > FIND:
                            with pe.If(rounds > 1):
                                with pe.Fori(1, rounds):
                                    with pe.Fori(0, deals):
                                        deal_out()
                                    pe.reg_add(turn, turn, 1)
                    with pe.Else():
                        pe.reg_add(turn, turn, 1)
                words_of(0, 0)
                words_of(1, 1)
                with pe.Fori(0, T2 - 1) as j:
                    for i in (2, 3):
                        words_of(2 * j + i, i % 2)
                deal_out()
                further_deals(T - 2)
                counts_of(T - 1, 1)
                deal_out()
                further_deals(T - 1)

            def attend(layer):
                def group(S, r, b, first_of=None):
                    u = pe.snap(unit[r])
                    if first_of is not None and not (isinstance(first_of, int) and first_of == NP - 1):
                        spread_query(first_of + 1, 1 - b)
                    pe.wait_ge(s_kr[r], u)
                    for i in range(S.n):
                        ins = pe.transpose(kT[b][:, i, :], kr[:, b, i, :], ident[:, :])
                    ins.then_inc(s_kT[r], 1)
                    pe.wait_ge(s_mb[r], u)
                    for i in range(S.n):
                        ins = pe.matmul(mrep[b][:, i, :], mb[:, b, i, :], ident[:, :], start=True, stop=True)
                    ins.then_inc(s_mrep[r], 1)
                    pe.wait_ge(s_p[r], u)
                    weights = S.cells(pr[:, b])
                    for i in range(S.n):
                        for s in range(S.G):
                            ins = pe.matmul(prod[b][:, i, :], weights[:, i, s, :], rows[:, r, i * S.G + s, 0:VW],
                                            start=(s == 0), stop=(s == S.G - 1))
                    ins.then_inc(s_pv[r], 1)
                    pe.reg_add(unit[r], unit[r], 1)

                def spread_query(p, b):
                    pe.wait_ge(s_qb, layer * NP + p + 1)
                    for i in range(Tiles(p).n):
                        ins = pe.matmul(qrep[b][:, i, :], qb[:, b, i, :], ident[:, :], start=True, stop=True)
                    ins.then_inc(s_qrep, 1)

                def body(p, S, r, b):
                    if isinstance(p, int) and p == 0:
                        spread_query(0, 0)
                    group(S, r, b, p)
                    if T > S.G:
                        n = pe.value_load(npair[0:1, bass.ds(p, 1)], min_val=1, max_val=T)
                        with pe.If(n > S.G):
                            with pe.Fori(1, (n + S.G - 1) // S.G) as g:
                                group(S, r, b)

                each_set(pe, body)

            credit(pe, *s_hT, *s_pack, *s_pv)
            weights()
            project(0)
            pack()
            attend(0)
            project(1)
            attend(1)


def kernel(x, adj, L0_gnn_W, L0_gnn_a, L1_gnn_W, L1_gnn_a):
    import concourse.bacc as bacc
    from concourse.bass_utils import run_bass_kernel_spmd

    x, adj = np.ascontiguousarray(x), np.ascontiguousarray(adj)
    T = x.shape[0] // P
    i = np.arange(P)
    code = np.where(i[:, None] // WORD == np.arange(NW)[None, :], 2.0 ** (i[:, None] % WORD), 0.0).astype(np.float32)
    arrays = {
        "in_x": x, "in_adj": adj,
        "in_W0": np.ascontiguousarray(L0_gnn_W), "in_a0": np.ascontiguousarray(L0_gnn_a),
        "in_W1": np.ascontiguousarray(L1_gnn_W), "in_a1": np.ascontiguousarray(L1_gnn_a).reshape(-1),
        "c_ident": np.eye(P, dtype=np.float32),
        "c_code": code,
        "c_bitmask": np.broadcast_to((1 << (i % WORD)).astype(np.uint16), (P, P)).copy(),
        "c_block": np.broadcast_to(((np.arange(T) + 1) * BLOCK_CODE).astype(np.float32), (P, T)).copy(),
        "c_lane": (i - P).astype(np.float32).reshape(P, 1),
        "c_iota": np.broadcast_to(i.astype(np.float32), (P, P)).copy(),
        "c_before": (i[:, None] < i[None, :]).astype(np.float32),
    }
    nc = bacc.Bacc("TRN2", target_bir_lowering=False, num_devices=1)
    args = [nc.dram_tensor(k, a.shape, mybir.dt.from_np(a.dtype), kind="ExternalInput").ap() for k, a in arrays.items()]
    out = nc.dram_tensor("out_x", x.shape, F32, kind="ExternalOutput").ap()
    gat_two_layers(nc, *args, out)
    return run_bass_kernel_spmd(nc, [arrays], core_ids=[0]).results[0]["out_x"]
```

```python
from contextlib import ExitStack

import numpy as np
import concourse.bass as bass
from concourse import mybir
from concourse.alu_op_type import AluOpType as ALU

ACT = mybir.ActivationFunctionType
AX = mybir.AxisListType
F32 = mybir.dt.float32
BF16 = mybir.dt.bfloat16
I32 = mybir.dt.int32
U16 = mybir.dt.uint16

P = 128
WORD = 16
NW = P // WORD
FIND = 8
DEAL = 6
OPENING = ((1, 13), (2, 6), (3, 5), (2, 4), (4, 3), (4, 3))
Q, SLIM = 4, 2
CELLS = 16
RING = 4
CH = 4
EPS = 1e-5
ALPHA = 0.2
MASKED = -1e30
FLOOR = -1e28
BLOCK_CODE = 1 << WORD
CONSTANTS = 7


class Chain:

    def __init__(self, eng, sem):
        self.eng, self.sem, self.n = eng, sem, 0

    def done(self, ins):
        ins.then_inc(self.sem, 1)
        self.n += 1

    def wait(self):
        self.eng.wait_ge(self.sem, self.n)

    def link(self, ins):
        self.done(ins)
        self.wait()

    def restart(self):
        if self.n:
            self.wait()
            self.eng.sem_clear(self.sem)
            self.n = 0


def gat_two_layers(nc, x, adj, W0, a0, W1, a1, ident_c, code_c, bitmask_c, block_c, lane_c, iota_c, before_c, out):
    N, F = x.shape
    T = N // P
    T2 = T // 2
    NC2 = T // CH // 2
    LD = 4
    LW = N // LD
    BY_SCALAR = (1, 2)
    LB = LW // P
    VW = F + 3
    QC, KC, ONE = F, F + 1, F + 2
    VS = VW + 1
    opening = [o for k, o in enumerate(OPENING) if sum(n for n, _ in OPENING[:k + 1]) <= T]
    first_alike = sum(n for n, _ in opening)
    NO = len(opening)
    NP = NO + (T - first_alike) // Q
    SL = max(-(-T // g) * g for g in [SLIM, DEAL] + [g for _, g in opening])
    PW = NW + 1
    NG = -(-T // SLIM)

    table = nc.dram_tensor("value_table", [N, VS], F32, kind="Internal").ap()
    x1 = nc.dram_tensor("x_between_layers", [N, F], F32, kind="Internal").ap()
    layer_in, layer_out = [x, x1], [x1, out]

    with ExitStack() as ctx:
        def sb(name, shape, dt=F32):
            return ctx.enter_context(nc.sbuf_tensor(name, shape, dt))

        def sem(name):
            return ctx.enter_context(nc.semaphore(name))

        def sem2(name):
            return [sem(f"{name}{i}") for i in range(2)]

        ident = sb("ident", [P, P])
        ones = sb("ones", [P, P])
        code_f = sb("code_f", [P, NW])
        code = sb("code", [P, NW], BF16)
        bitmask = sb("bitmask", [P, P], U16)
        blockcode = sb("blockcode", [P, T])
        lane = sb("lane", [P, 1])
        iota = sb("iota", [P, P])
        lanes_before = sb("lanes_before", [P, P])
        Wx = [sb(f"Wx{l}", [P, F + 2]) for l in range(2)]
        acol = [sb(f"acol{l}", [P, 2]) for l in range(2)]
        WT = sb("WT", [P, P])
        xin = sb("xin", [P, 2, CH, F])
        stat = sb("stat", [P, 2, 4, CH])
        hrow = sb("hrow", [P, 2, CH, F])
        vrow = sb("vrow", [P, 2, CH, VS])
        vsum = sb("vsum", [P, CH, VS])
        qcol = sb("qcol", [P, T])
        sumrep = sb("sumrep", [P, VS])
        gathered = sb("gathered", [P, max(RING * CELLS * VS, LD * LW)])
        rows = gathered[:, 0:RING * CELLS * VS].rearrange("p (r c w) -> p r c w", r=RING, c=CELLS)
        adj_in = gathered[:, 0:LD * LW].bitcast(I32).rearrange("p (k n) -> p k n", k=LD)
        occ = sb("occ", [P, T])
        occ01 = sb("occ01", [P, T])
        base = sb("base", [P, T])
        cnt = sb("cnt", [P, 2])
        top = sb("top", [P, 2, NW, FIND])
        topi = sb("topi", [P, NW, FIND], I32)
        rank = sb("rank", [P, 1])
        unused = sb("unused", [P, FIND])
        place = sb("place", [P, FIND], I32)
        to_lane = sb("to_lane", [P, FIND], I32)
        to_slot = sb("to_slot", [P, FIND], I32)
        at_slot = sb("at_slot", [P, FIND, DEAL])
        item = sb("item", [P, FIND, PW])
        items = sb("items", [P, FIND, DEAL, PW])
        dealt = sb("dealt", [P, SL, PW])
        total = sb("total", [1, 2], I32)
        words = sb("words", [P, T, SL, NW], U16)
        idx = sb("idx", [P, T, SL], U16)
        nfind = sb("nfind", [1, T], I32)
        nslots = sb("nslots", [1, T], I32)
        nset = sb("nset", [1, NP], I32)
        ngather = sb("ngather", [1, NG, NP], I32)
        load = sb("load", [1, T], I32)
        idxs = sb("idxs", [P, RING, CELLS], I32)
        bits = sb("bits", [P, CELLS * P], U16)
        sc = sb("sc", [P, 2, CELLS * P])
        pr = sb("pr", [P, 2, CELLS * P])
        scratch = sc[:, :, :].rearrange("p b c -> p (b c)")
        at_lane = scratch[:, FIND * P:2 * FIND * P].rearrange("p (s i) -> p s i", s=FIND)
        codes = scratch[:, 2 * FIND * P:2 * FIND * P + 2 * NW * T].rearrange("p (b w c) -> p b w c", b=2, w=NW)
        cen = scratch[:, 2 * FIND * P:2 * FIND * P + 2 * CH * F].rearrange("p (b q f) -> p b q f", b=2, q=CH)
        squares = scratch[:, 0:2 * CH * F].rearrange("p (b q f) -> p b q f", b=2, q=CH)
        gsum = scratch[0:1, 3 * FIND * P:]
        a01 = pr[:, :, :].rearrange("p b c -> p (b c)")[:, 0:N // 2].bitcast(BF16).rearrange("p (k n) -> p k n", k=LD)
        hT = pr[:, :, 0:CH * P]
        kr = sb("kr", [P, 2, Q, P])
        qb = sb("qb", [P, 2, Q, P])
        mb = sb("mb", [P, 2, Q, P])
        found = sb("found", [P, 2, Q])
        m_run = sb("m_run", [P, 2, Q])
        m_new = sb("m_new", [P, 2, Q])
        m_fall = sb("m_fall", [P, 2, Q])
        corr = sb("corr", [P, 2, Q])
        acc = sb("acc", [P, 2, Q, VW])
        empty = sb("empty", [P, 2, Q])
        den = sb("den", [P, 2, Q])
        num = sb("num", [P, 2, Q, F])
        hmin = sb("hmin", [P, 2, Q, F])
        xres = sb("xres", [P, 2, Q, F])
        obuf = sb("obuf", [P, 2, Q, F])

        ps = ctx.enter_context(nc.psum_tensor("ps", [P, 8, 512], F32))

        kT = [ps[:, b, :].rearrange("p (t i) -> p t i", t=Q) for b in range(2)]
        mrep = kT
        qrep = [ps[:, 2 + b, :].rearrange("p (t i) -> p t i", t=Q) for b in range(2)]
        prod = [ps[:, 4 + 2 * b:6 + 2 * b, :].rearrange("p k (t w) -> p (k t) w", t=Q // 2)[:, :, 0:VW] for b in range(2)]

        s_const, s_memset, s_W, s_init = sem("s_const"), sem("s_memset"), sem("s_W"), sem("s_init")
        s_wt, s_wts, s_wa, s_was = sem("s_wt"), sem("s_wts"), sem("s_wa"), sem("s_was")
        s_cen, s_var, s_std = sem2("s_cen"), sem2("s_var"), sem2("s_std")
        s_xin, s_h, s_hT, s_hTs = sem2("s_xin"), sem2("s_h"), sem2("s_hT"), sem2("s_hTs")
        s_wh, s_vrow, s_q, s_vs, s_tab = sem2("s_wh"), sem2("s_vrow"), sem2("s_q"), sem2("s_vs"), sem2("s_tab")
        s_sum, s_sumrep = sem("s_sum"), sem("s_sumrep")
        s_adj = [sem(f"s_adj{i}") for i in range(LD)]
        s_conv = [sem(f"s_conv{i}") for i in range(LD)]
        s_pack = [sem(f"s_pack{i}") for i in range(LD)]
        s_code, s_cntT, s_occ, s_cnt = sem2("s_code"), sem2("s_cntT"), sem("s_occ"), sem("s_cnt")
        s_relu, s_lane, s_items, s_dealt = sem("s_relu"), sem("s_lane"), sem("s_items"), sem("s_dealt")
        s_slots, s_packed, s_counted = sem("s_slots"), sem("s_packed"), sem("s_counted")
        s_idx, s_rows, s_zq = [[sem(f"{n}{r}") for r in range(RING)] for n in ("s_idx", "s_rows", "s_zq")]
        s_kr, s_kT, s_mb, s_mrep = [[sem(f"{n}{r}") for r in range(RING)] for n in ("s_kr", "s_kT", "s_mb", "s_mrep")]
        s_d, s_p, s_pv, s_fall, s_corr = [[sem(f"{n}{r}") for r in range(RING)] for n in ("s_d", "s_p", "s_pv", "s_fall", "s_corr")]
        s_qb, s_qrep, s_hmin, s_em, s_fin = sem("s_qb"), sem("s_qrep"), sem("s_hmin"), sem("s_em"), sem("s_fin")
        s_xres, s_out = sem2("s_xres"), sem2("s_out")
        s_held = sem("s_held")
        s_vchain, s_gchain = sem("s_vchain"), sem("s_gchain")

        class Tiles:

            def __init__(self, p):
                if isinstance(p, int) and p < NO:
                    self.first, (self.n, self.G) = sum(n for n, _ in opening[:p]), opening[p]
                else:
                    self.first, self.n, self.G = p * Q - (NO * Q - first_alike), Q, SLIM

            def cells(self, flat):
                return flat[:, 0:self.n * self.G * P].rearrange("p (t s i) -> p t s i", t=self.n, s=self.G)

        def each_set(eng, body):
            p = 0
            while p < NP:
                rounds = (NP - 2 - p) // RING if p > NO else 0
                if rounds < 1:
                    body(p, Tiles(p), p % RING, p % 2)
                    p += 1
                    continue
                with eng.Fori(0, rounds) as j:
                    for i in range(p, p + RING):
                        body(j * RING + i, Tiles(j * RING + i), i % RING, i % 2)
                p += rounds * RING

        def registers(eng, name, start):
            regs = [eng.alloc_register(f"{name}{r}") for r in range(RING)]
            for r in regs:
                eng.reg_mov(r, start)
            return regs

        def chunk(dram, c):
            return dram[bass.ds(c * (CH * P), CH * P), :].rearrange("(q p) f -> p q f", p=P)

        def credit(eng, *sems):
            for s in sems:
                eng.sem_inc(s, 1)

        def hold(eng, s, value):
            eng.wait_ge(s, value)
            eng.sem_inc(s_held, 1)

        block = ctx.enter_context(nc.Block())

        @block.sync
        def _(sp):
            for dst, src in ((ident, ident_c), (code_f, code_c), (bitmask, bitmask_c), (blockcode, block_c),
                             (lane, lane_c), (iota, iota_c), (lanes_before, before_c)):
                sp.dma_start(dst[:, :], src).then_inc(s_const, 16)
            for l, (W, a) in enumerate(((W0, a0), (W1, a1))):
                sp.dma_start(Wx[l][:, 0:F], W).then_inc(s_W, 16)
                with nc.allow_non_contiguous_dma(reason="256 numbers"):
                    sp.dma_start(acol[l][:, :], a.rearrange("(s p) -> p s", p=P)).then_inc(s_W, 16)

            def load_x(layer):
                with sp.Fori(0, NC2) as cc:
                    for b in range(2):
                        sp.wait_ge(s_cen[b], layer * NC2 + cc + 1)
                        sp.dma_start(xin[:, b], chunk(layer_in[layer], 2 * cc + b)).then_inc(s_xin[b], 16)

            def load_adj():
                with sp.Fori(0, T2) as tt:
                    for b in range(2):
                        t = 2 * tt + b
                        for k in range(LD):
                            sp.wait_ge(s_conv[k], t + 1)
                            sp.dma_start(adj_in[:, k], adj[bass.ds(t * P, P), k * LW:(k + 1) * LW]).then_inc(s_adj[k], 16)

            def rows_of(dram, S):
                return dram[bass.ds(S.first * P, S.n * P), :].rearrange("(t i) f -> i t f", t=S.n)

            def residual_and_store(layer):
                def store(p, b):
                    sp.wait_ge(s_fin, layer * NP + p + 3)
                    S = Tiles(p)
                    sp.dma_start(rows_of(layer_out[layer], S), obuf[:, b, 0:S.n]).then_inc(s_out[b], 16)

                def body(p, S, r, b):
                    sp.wait_ge(s_fin, layer * NP + p + 1)
                    sp.dma_start(xres[:, b, 0:S.n], rows_of(layer_in[layer], S)).then_inc(s_xres[b], 16)
                    if isinstance(p, int) and p == 0:
                        return
                    store(p - 1, 1 - b)

                each_set(sp, body)
                store(NP - 1, 1)
                for b in range(2):
                    sp.wait_ge(s_out[b], 16 * (NP // 2) * (layer + 1))

            load_x(0)
            load_adj()
            residual_and_store(0)
            load_x(1)
            residual_and_store(1)

        @block.gpsimd
        def _(pool):
            chain = Chain(pool, s_gchain)
            unit = registers(pool, "pool_unit", 1)

            def sum_values(layer):
                chain.link(pool.memset(vsum[:, :, :], 0.0))
                chain.restart()
                with pool.Fori(0, NC2) as cc:
                    for b in range(2):
                        pool.wait_ge(s_vrow[b], layer * NC2 + cc + 2)
                        ins = pool.tensor_tensor(vsum[:, :, 0:VW], vsum[:, :, 0:VW], vrow[:, b, :, 0:VW], ALU.add)
                        chain.link(ins)
                        pool.sem_inc(s_vs[b], 1)
                    chain.restart()

            def gather(layer):
                for b in range(2):
                    pool.wait_ge(s_tab[b], 16 * NC2 * (layer + 1))

                def gather_group(S, r, g):
                    u = pool.snap(unit[r])
                    hold(pool, s_pv[r], u)
                    c = S.n * S.G
                    pool.tensor_copy(idxs[:, r, 0:c].rearrange("p (t s) -> p t s", t=S.n),
                                     idx[:, bass.ds(S.first, S.n), bass.ds(g * S.G, S.G)]).then_inc(s_idx[r], 1)
                    n = [pool.value_load(nslots[0:1, bass.ds(S.first + i, 1)], min_val=1, max_val=T) for i in range(S.n)]
                    hold(pool, s_idx[r], u)
                    for i in range(S.n):
                        for s in range(S.G):
                            at = i * S.G + s
                            with pool.If(n[i] > g * S.G + s):
                                pool.indirect_dma_start(
                                    out=rows[:, r, at, :], out_offset=None, in_=table[:, :],
                                    in_offset=bass.IndirectOffsetOnAxis(ap=idxs[:, r, at:at + 1], axis=0),
                                ).then_inc(s_rows[r], 16)
                    pool.reg_add(unit[r], unit[r], 1)

                def body(p, S, r, b):
                    if isinstance(p, int) and p < RING:
                        pool.wait_ge(s_packed, p + 1)
                    n = pool.value_load(nset[0:1, bass.ds(p, 1)], min_val=1, max_val=T)
                    with pool.Fori(0, (n + S.G - 1) // S.G) as g:
                        gather_group(S, r, g)

                each_set(pool, body)

            credit(pool, *s_vs)
            pool.memset(words[:, :, :, :], 2 ** WORD - 1).then_inc(s_slots, 1)
            pool.memset(idx[:, :, :], 0).then_inc(s_slots, 1)
            pool.wait_ge(s_init, 1)
            sum_values(0)
            pool.wait_ge(s_packed, 1)
            gather(0)
            sum_values(1)
            gather(1)

        @block.scalar
        def _(act):
            unit = registers(act, "act_unit", 1)
            landed = registers(act, "act_landed", 0)

            def project(layer):
                def roots(cc, b):
                    c = layer * NC2 + cc
                    act.wait_ge(s_cen[b], c + 2)
                    for q in range(CH):
                        ins = act.activation(squares[:, b, q, :], cen[:, b, q, :], ACT.Square, accum_out=stat[:, b, 1, q:q + 1])
                    ins.then_inc(s_var[b], 1)
                    act.wait_ge(s_var[b], c + 1)
                    act.activation(stat[:, b, 2, :], stat[:, b, 1, :], ACT.Sqrt, bias=EPS, scale=1.0 / F).then_inc(s_std[b], 1)

                def transposed(cc, b):
                    act.wait_ge(s_hT[b], layer * NC2 + cc + 2)
                    act.activation(hT[:, b, :], ps[:, b, :], ACT.Copy).then_inc(s_hTs[b], 1)

                def values(cc, b):
                    c = layer * NC2 + cc
                    if isinstance(c, int):
                        if c:
                            act.wait_ge(s_tab[b], 16 * c)
                    else:
                        with act.If(c > 0):
                            hold(act, s_tab[b], 16 * c)
                    act.wait_ge(s_wh[b], c + 1)
                    act.wait_ge(s_vs[b], c + 1)
                    act.wait_ge(s_q[b], c + 1)
                    wh = ps[:, 2 + 2 * b:4 + 2 * b, :].rearrange("p k (h w) -> p (k h) w", h=2)
                    act.activation(vrow[:, b, :, 0:F + 2], wh[:, :, 0:F + 2], ACT.Copy).then_inc(s_vrow[b], 1)
                    act.wait_ge(s_vrow[b], c + 2)
                    act.activation(qcol[:, bass.ds((2 * cc + b) * CH, CH)], vrow[:, b, :, QC], ACT.Copy).then_inc(s_q[b], 1)
                    act.dma_start(chunk(table, 2 * cc + b), vrow[:, b]).then_inc(s_tab[b], 16)

                roots(0, 0)
                roots(0, 1)
                transposed(0, 0)
                with act.Fori(0, NC2 - 1) as cc:
                    roots(cc + 1, 0)
                    transposed(cc, 1)
                    values(cc, 0)
                    roots(cc + 1, 1)
                    transposed(cc + 1, 0)
                    values(cc, 1)
                transposed(NC2 - 1, 1)
                values(NC2 - 1, 0)
                values(NC2 - 1, 1)

            def attend(layer):
                def score(p, S, r, b, g):
                    more = act.value_load(ngather[0:1, bass.ds(g, 1), bass.ds(p, 1)], min_val=0, max_val=16 * S.n * S.G)
                    act.reg_add(landed[r], landed[r], more)
                    act.wait_ge(s_rows[r], act.snap(landed[r]))
                    for i in range(S.n):
                        for s in range(S.G):
                            ins = act.activation(S.cells(sc[:, b])[:, i, s, :], qrep[b][:, i, :], ACT.Identity,
                                                 bias=rows[:, r, i * S.G + s, KC:KC + 1])
                    ins.then_inc(s_zq[r], 1)

                def spread_query(S, b):
                    act.activation(qb[:, b, 0:S.n], qcol[:, bass.ds(S.first, S.n)][:, :, None].to_broadcast([P, S.n, P]),
                                   ACT.Copy).then_inc(s_qb, 1)

                def exponential(S, r, b):
                    act.activation(pr[:, b, 0:S.n * S.G * P], sc[:, b, 0:S.n * S.G * P], ACT.Exp).then_inc(s_p[r], 1)

                def exponentials(S, r, b):
                    u = act.snap(unit[r])
                    act.wait_ge(s_d[r], u)
                    exponential(S, r, b)
                    act.sem_inc(s_corr[r], 1)
                    act.reg_add(unit[r], unit[r], 1)

                def later_groups(p, S, r, b, n):
                    with act.Fori(1, (n + S.G - 1) // S.G) as g:
                        score(p, S, r, b, g)
                        u = act.snap(unit[r])
                        act.wait_ge(s_fall[r], u)
                        act.activation(corr[:, b, 0:S.n], m_fall[:, b, 0:S.n], ACT.Exp).then_inc(s_corr[r], 1)
                        act.wait_ge(s_d[r], u)
                        act.wait_ge(s_pv[r], u)
                        exponential(S, r, b)
                        act.reg_add(unit[r], unit[r], 1)

                def first_score(p, S, r, b):
                    act.wait_ge(s_qrep, layer * NP + p + 1)
                    score(p, S, r, b, 0)
                    if not (isinstance(p, int) and p == NP - 1):
                        spread_query(Tiles(p + 1), 1 - b)

                def elu_exponential(p, S, b):
                    act.wait_ge(s_hmin, layer * NP + p + 1)
                    act.activation(hmin[:, b, 0:S.n], hmin[:, b, 0:S.n], ACT.Exp).then_inc(s_em, 1)

                def body(p, S, r, b):
                    if isinstance(p, int) and p == 0:
                        spread_query(S, 0)
                        first_score(p, S, r, b)
                        return
                    r1, b1, S1 = (r - 1) % RING, 1 - b, Tiles(p - 1)
                    if T <= S1.G:
                        first_score(p, S, r, b)
                        exponentials(S1, r1, b1)
                        elu_exponential(p - 1, S1, b1)
                        return
                    n = act.value_load(nset[0:1, bass.ds(p - 1, 1)], min_val=1, max_val=T)
                    with act.If(n > S1.G):
                        exponentials(S1, r1, b1)
                        later_groups(p - 1, S1, r1, b1, n)
                        first_score(p, S, r, b)
                    with act.Else():
                        first_score(p, S, r, b)
                        exponentials(S1, r1, b1)
                    elu_exponential(p - 1, S1, b1)

                each_set(act, body)
                r, b, S = (NP - 1) % RING, (NP - 1) % 2, Tiles(NP - 1)
                exponentials(S, r, b)
                if T > S.G:
                    n = act.value_load(nset[0:1, NP - 1:NP], min_val=1, max_val=T)
                    with act.If(n > S.G):
                        later_groups(NP - 1, S, r, b, n)
                elu_exponential(NP - 1, S, b)

            def pack():
                def count(t, b):
                    act.wait_ge(s_occ, t + 1)
                    act.activation(occ01[:, :], occ[:, :], ACT.Sign, accum_out=cnt[:, b:b + 1]).then_inc(s_cnt, 1)

                def convert(t):
                    for i, k in enumerate(BY_SCALAR):
                        act.wait_ge(s_adj[k], 16 * (t + 1))
                        act.wait_ge(s_pack[k], t + 1)
                        act.activation(a01[:, k, :], adj_in[:, k, :], ACT.Relu).then_inc(s_relu, 1)
                        act.wait_ge(s_relu, 2 * t + i + 1)
                        act.activation(a01[:, k, :], a01[:, k, :], ACT.Sign).then_inc(s_conv[k], 1)

                convert(0)
                count(0, 0)
                convert(1)
                with act.Fori(0, T2 - 1) as j:
                    for i in (2, 3):
                        count(2 * j + i - 1, (i - 1) % 2)
                        convert(2 * j + i)
                count(T - 1, 1)

            credit(act, *s_hTs, *s_vrow, *s_q)
            project(0)
            pack()
            act.wait_ge(s_counted, 1)
            attend(0)
            project(1)
            attend(1)


        @block.vector
        def _(dve):
            chain = Chain(dve, s_vchain)
            unit = registers(dve, "dve_unit", 1)

            def init():
                dve.memset(ones[:, :], 1.0).then_inc(s_memset, 1)
                chain.done(dve.memset(vrow[:, :, :, VW - 1:VS], 1.0))
                chain.done(dve.memset(acc[:, :, :, :], 0.0))
                dve.wait_ge(s_const, 16 * CONSTANTS)
                chain.link(dve.tensor_copy(code[:, :], code_f[:, :]))
                dve.sem_inc(s_init, 1)
                for l in range(2):
                    dve.wait_ge(s_wt, l + 1)
                    dve.tensor_copy(WT[:, :], ps[:, 0, 0:P]).then_inc(s_wts, 1)
                    dve.wait_ge(s_wa, l + 1)
                    qh = 1 - l
                    dve.tensor_copy(Wx[l][:, F:F + 1], ps[:, 1, qh:qh + 1]).then_inc(s_was, 1)
                    dve.tensor_copy(Wx[l][:, F + 1:F + 2], ps[:, 1, 1 - qh:2 - qh]).then_inc(s_was, 1)
                chain.restart()

            def layernorm(layer):
                def centre(cc, b):
                    c = layer * NC2 + cc
                    xb, cb = xin[:, b], cen[:, b]
                    total, mean = stat[:, b, 3, :], stat[:, b, 0, :]
                    dve.wait_ge(s_h[b], c + 1)
                    dve.wait_ge(s_xin[b], 16 * (c + 1))
                    chain.link(dve.tensor_reduce(total, xb, AX.X, ALU.add))
                    chain.link(dve.tensor_scalar(mean, total, 1.0 / F, None, ALU.mult))
                    dve.tensor_tensor(cb, xb, stat[:, b, 0, :, None].to_broadcast([P, CH, F]), ALU.subtract).then_inc(s_cen[b], 1)

                def scale(cc, b):
                    dve.wait_ge(s_std[b], layer * NC2 + cc + 1)
                    dve.wait_ge(s_hT[b], layer * NC2 + cc + 1)
                    chain.link(dve.reciprocal(stat[:, b, 3, :], stat[:, b, 2, :]))
                    dve.scalar_tensor_tensor(hrow[:, b], cen[:, b], 0.0, stat[:, b, 3, :, None].to_broadcast([P, CH, F]),
                                             ALU.max, ALU.mult).then_inc(s_h[b], 1)

                centre(0, 0)
                chain.restart()
                with dve.Fori(0, NC2 - 1) as cc:
                    centre(cc, 1)
                    scale(cc, 0)
                    centre(cc + 1, 0)
                    scale(cc, 1)
                    chain.restart()
                centre(NC2 - 1, 1)
                scale(NC2 - 1, 0)
                scale(NC2 - 1, 1)
                chain.restart()

            def value_sums(layer):
                dve.wait_ge(s_sum, layer + 1)
                dve.tensor_copy(sumrep[:, 0:VW], ps[:, 7, 0:VW]).then_inc(s_sumrep, 1)
                dve.wait_ge(s_sumrep, layer + 1)

            deal = registers(dve, "dve_deal", 1)[0]

            def places(b):
                chain.link(dve.tensor_scalar(unused[:, :], iota[:, 0:FIND], cnt[:, b:b + 1], float(T * P), ALU.is_ge, ALU.mult))
                chain.link(dve.scalar_tensor_tensor(place[:, :], iota[:, 0:FIND], rank[:, 0:1], unused[:, :], ALU.add, ALU.add))
                chain.done(dve.tensor_scalar(to_lane[:, :], place[:, :], P - 1, None, ALU.bitwise_and))
                chain.done(dve.tensor_scalar(to_slot[:, :], place[:, :], P.bit_length() - 1, None, ALU.logical_shift_right))
                chain.wait()
                dve.tensor_tensor(at_lane[:, :, :], to_lane[:, :, None].to_broadcast([P, FIND, P]),
                                  iota[:, None, :].to_broadcast([P, FIND, P]), ALU.is_equal).then_inc(s_lane, 1)

            def largest(b):
                for w in range(NW):
                    chain.done(dve.max(top[:, b, w, :], codes[:, b, w, :]))

            def decode(b):
                chain.link(dve.tensor_copy(topi[:, :, :], top[:, b]))
                parts = topi[:, :, :].bitcast(U16).rearrange("p w (s h) -> p s w h", h=2)
                chain.done(dve.tensor_copy(item[:, :, 0:NW], parts[:, :, :, 0]))
                chain.done(dve.tensor_scalar(item[:, :, NW], parts[:, :, 0, 1], float(P), lane[:, 0:1], ALU.mult, ALU.add))

            def send_items():
                chain.link(dve.tensor_tensor(at_slot[:, :, :], to_slot[:, :, None].to_broadcast([P, FIND, DEAL]),
                                             iota[:, None, 0:DEAL].to_broadcast([P, FIND, DEAL]), ALU.is_equal))
                dve.tensor_tensor(items[:, :, :, :], item[:, :, None, :].to_broadcast([P, FIND, DEAL, PW]),
                                  at_slot[:, :, :, None].to_broadcast([P, FIND, DEAL, PW]), ALU.mult).then_inc(s_items, 1)

            def take_dealt():
                dve.wait_ge(s_dealt, dve.snap(deal))
                dve.reg_add(deal, deal, 1)

            def dealt_at(e):
                return dealt[:, bass.ds(e * DEAL, DEAL), :]

            dealt_ps = ps[:, 4, 0:DEAL * PW].rearrange("p (s w) -> p s w", s=DEAL)

            def keep_dealt(t, e):
                chain.done(dve.tensor_scalar(words[:, bass.ds(t, 1), bass.ds(e * DEAL, DEAL), :].rearrange("p t s w -> p (t s) w"),
                                             dealt_at(e)[:, :, 0:NW], -1.0, float(2 ** WORD - 1), ALU.mult, ALU.add))
                chain.done(dve.tensor_copy(idx[:, bass.ds(t, 1), bass.ds(e * DEAL, DEAL)].rearrange("p t s -> p (t s)"),
                                           dealt_at(e)[:, :, NW]))

            def next_deal():
                chain.link(dve.tensor_scalar(to_slot[:, :], to_slot[:, :], -float(DEAL), None, ALU.add))

            def further_deals(t, b):
                n = dve.value_load(load[0:1, bass.ds(t, 1)], min_val=0, max_val=2 * T)
                chain.restart()
                with dve.If(n > FIND):
                    rounds = (dve.value_load(nfind[0:1, bass.ds(t, 1)], min_val=0, max_val=T) + FIND - 1) // FIND
                    deals = (dve.value_load(nslots[0:1, bass.ds(t, 1)], min_val=1, max_val=T) + DEAL - 1) // DEAL
                    with dve.If(deals > 1):
                        with dve.Fori(1, deals) as e:
                            next_deal()
                            send_items()
                            take_dealt()
                            chain.link(dve.tensor_copy(dealt_at(e), dealt_ps))
                            chain.restart()
                    if T > FIND:
                        with dve.If(rounds > 1):
                            with dve.Fori(1, rounds):
                                for w in range(NW):
                                    chain.done(dve.match_replace(codes[:, b, w, :], top[:, b, w, :], codes[:, b, w, :], 0.0))
                                more = cnt[:, b:b + 1]
                                chain.done(dve.tensor_scalar(more, more, -float(FIND), None, ALU.add))
                                chain.done(dve.tensor_scalar(rank[:, :], rank[:, :], float(FIND), None, ALU.add))
                                chain.wait()
                                places(b)
                                largest(b)
                                chain.wait()
                                decode(b)
                                chain.restart()
                                with dve.Fori(0, deals) as e:
                                    send_items()
                                    take_dealt()
                                    chain.done(dve.tensor_tensor(dealt_at(e), dealt_at(e), dealt_ps, ALU.add))
                                    next_deal()
                                    chain.restart()
                    with dve.If(deals > 1):
                        with dve.Fori(1, deals) as e:
                            keep_dealt(t, e)
                            chain.restart()

            def pack():
                def convert(t, k):
                    dve.wait_ge(s_adj[k], 16 * (t + 1))
                    dve.wait_ge(s_pack[k], t + 1)
                    dve.tensor_scalar(a01[:, k, :], adj_in[:, k, :], 0.0, None, ALU.is_gt).then_inc(s_conv[k], 1)

                def count_slots(t, b):
                    pc = ps[:, 2 + b, :]
                    dve.wait_ge(s_cntT[b], t // 2 + 1)
                    with nc.allow_low_precision(reason="small whole numbers"):
                        chain.done(dve.tensor_reduce(nfind[0:1, bass.ds(t, 1)], pc[0:1, 0:P], AX.X, ALU.max))
                    chain.done(dve.tensor_scalar(total[:, 0:1], pc[0:1, P + 1:P + 2], float(P - 1), None, ALU.add))
                    chain.done(dve.tensor_copy(rank[:, :], pc[:, P:P + 1]))
                    chain.wait()
                    chain.link(dve.tensor_scalar(total[:, 1:2], total[:, 0:1], P.bit_length() - 1, None, ALU.logical_shift_right))
                    chain.link(dve.tensor_scalar(nslots[0:1, bass.ds(t, 1)], total[:, 1:2], 1.0, None, ALU.max))
                    chain.done(dve.scalar_tensor_tensor(load[0:1, bass.ds(t, 1)], total[:, 1:2], float(FIND - DEAL), nfind[0:1, bass.ds(t, 1)],
                                                        ALU.add, ALU.max))

                def keep_slots(t, b):
                    take_dealt()
                    chain.link(dve.tensor_copy(dealt_at(0), dealt_ps))
                    if T > min(FIND, DEAL):
                        further_deals(t, b)
                    keep_dealt(t, 0)

                def body(t, b, before, after):
                    pk = ps[:, 1 - b, 0:T * NW]
                    if after:
                        convert(t, 0)
                    if before:
                        for k in range(LD):
                            dve.wait_ge(s_pack[k], t + 1)
                        if not isinstance(t, int) or t > 1:
                            dve.wait_ge(s_cnt, t - 1)
                        dve.tensor_reduce(occ[:, :], pk.rearrange("p (c w) -> p c w", w=NW), AX.X, ALU.max).then_inc(s_occ, 1)
                        dve.wait_ge(s_occ, t)
                        chain.link(dve.scalar_tensor_tensor(base[:, :], occ[:, :], 0.0, blockcode[:, :], ALU.is_gt, ALU.mult))
                        dve.tensor_tensor(codes[:, 1 - b], pk.rearrange("p (c w) -> p w c", w=NW),
                                          base[:, None, :].to_broadcast([P, NW, T]), ALU.add).then_inc(s_code[1 - b], 1)
                        hold(dve, s_code[1 - b], (t - 1) // 2 + 2)
                        largest(1 - b)
                        if not (isinstance(t, int) and t == 1):
                            keep_slots(t - 2, b)
                        count_slots(t - 1, 1 - b)
                        places(1 - b)
                        decode(1 - b)
                        chain.wait()
                        send_items()
                    if after:
                        convert(t, 3)
                    chain.restart()

                body(0, 0, False, True)
                body(1, 1, True, True)
                with dve.Fori(0, T2 - 1) as j:
                    for i in (2, 3):
                        body(2 * j + i, i % 2, True, True)
                body(T, 0, True, False)
                keep_slots(T - 1, 1)

                opened = [Tiles(p) for p in range(NO)]
                runs = [(S.first, S.first + S.n, p, S.n, S.G) for p, S in enumerate(opened)]
                if NP > NO:
                    runs.append((first_alike, T, NO, Q, SLIM))
                for t0, t1, p0, n, G in runs:
                    chain.done(dve.tensor_reduce(nset[:, p0:p0 + (t1 - t0) // n],
                                                 nslots[:, t0:t1].rearrange("o (p i) -> o p i", i=n), AX.X, ALU.max))
                chain.link(dve.memset(rows[:, 0], 0.0))
                dve.sem_inc(s_packed, 1)
                for t0, t1, p0, n, G in runs:
                    groups, sets = -(-T // G), (t1 - t0) // n
                    clip = scratch[0:1, 0:groups * (t1 - t0)].rearrange("o (g t) -> o g t", g=groups)
                    chain.link(dve.scalar_tensor_tensor(clip, iota[0:1, 0:groups, None].to_broadcast([1, groups, t1 - t0]), -float(G),
                                                        nslots[:, None, t0:t1].to_broadcast([1, groups, t1 - t0]), ALU.mult, ALU.add))
                    chain.link(dve.tensor_scalar(clip, clip, 0.0, float(G), ALU.max, ALU.min))
                    count = gsum[:, 0:groups * sets].rearrange("o (g p) -> o g p", g=groups)
                    chain.link(dve.tensor_reduce(count, clip.rearrange("o g (p i) -> o g p i", i=n), AX.X, ALU.add))
                    chain.link(dve.tensor_scalar(ngather[:, 0:groups, p0:p0 + sets], count, 16.0, None, ALU.mult))
                dve.sem_inc(s_counted, 1)
                for r in range(1, RING):
                    chain.link(dve.memset(rows[:, r], 0.0))
                    dve.sem_inc(s_packed, 1)
                chain.restart()

            def attend(layer):
                def mask_and_max(p, S, r, b, g):
                    u = dve.snap(unit[r])
                    c = S.n * S.G
                    wd = words[:, bass.ds(S.first, S.n), bass.ds(g * S.G, S.G), :].rearrange("p t s w -> p t (s w)")
                    chain.link(dve.tensor_tensor(
                        bits[:, 0:c * P].rearrange("p (t x j) -> p t x j", t=S.n, j=WORD),
                        wd[:, :, :, None].to_broadcast([P, S.n, S.G * NW, WORD]),
                        bitmask[:, None, None, 0:WORD].to_broadcast([P, S.n, S.G * NW, WORD]), ALU.bitwise_and))
                    dve.wait_ge(s_zq[r], u)
                    x = sc[:, b, 0:c * P]
                    chain.link(dve.scalar_tensor_tensor(x, bits[:, 0:c * P], MASKED, x, ALU.mult, ALU.add))
                    chain.link(dve.scalar_tensor_tensor(x, x, ALPHA, x, ALU.mult, ALU.max))
                    dve.tensor_reduce(kr[:, b, 0:S.n], S.cells(sc[:, b]).rearrange("p t s i -> p t i s"), AX.X, ALU.max).then_inc(s_kr[r], 1)

                def row_max(S, r, b, first):
                    u = dve.snap(unit[r])
                    run, new = m_run[:, b, 0:S.n], m_new[:, b, 0:S.n]
                    dve.wait_ge(s_kT[r], u)
                    chain.link(dve.tensor_reduce(found[:, b, 0:S.n], kT[b][:, 0:S.n], AX.X, ALU.max))
                    if first:
                        dve.memset(corr[:, b], 0.0).then_inc(s_fall[r], 1)
                        chain.link(dve.tensor_scalar(run, found[:, b, 0:S.n], FLOOR, None, ALU.max))
                    else:
                        chain.link(dve.tensor_tensor(new, found[:, b, 0:S.n], run, ALU.max))
                        dve.tensor_tensor(m_fall[:, b, 0:S.n], run, new, ALU.subtract).then_inc(s_fall[r], 1)
                        dve.wait_ge(s_fall[r], u)
                        chain.link(dve.tensor_copy(run, new))
                    dve.tensor_copy(mb[:, b, 0:S.n], run[:, :, None].to_broadcast([P, S.n, P])).then_inc(s_mb[r], 1)

                def less_max(S, r, b, later=False):
                    u = dve.snap(unit[r])
                    if later:
                        dve.wait_ge(s_corr[r], u)
                    dve.wait_ge(s_fall[r], u)
                    dve.wait_ge(s_mrep[r], u)
                    x = S.cells(sc[:, b])
                    dve.tensor_tensor(x, x, mrep[b][:, 0:S.n, None, :].to_broadcast([P, S.n, S.G, P]), ALU.subtract).then_inc(s_d[r], 1)
                    dve.reg_add(unit[r], unit[r], 1)

                def accumulate(S, r, b):
                    dve.wait_ge(s_pv[r], dve.snap(unit[r]))
                    for i in range(S.n):
                        chain.done(dve.scalar_tensor_tensor(acc[:, b, i, :], acc[:, b, i, :], corr[:, b, i:i + 1],
                                                            prod[b][:, i, :], ALU.mult, ALU.add))
                    chain.wait()

                def normalise(S, r, b):
                    accumulate(S, r, b)
                    total, miss, over, x = acc[:, b, 0:S.n, ONE], empty[:, b, 0:S.n], den[:, b, 0:S.n], num[:, b, 0:S.n]
                    chain.link(dve.tensor_scalar(miss, total, 0.0, None, ALU.is_equal))
                    chain.done(dve.scalar_tensor_tensor(over, miss, float(N), total, ALU.mult, ALU.add))
                    for i in range(S.n):
                        chain.done(dve.scalar_tensor_tensor(x[:, i, :], sumrep[:, 0:F], empty[:, b, i:i + 1],
                                                            acc[:, b, i, 0:F], ALU.mult, ALU.add))
                    chain.wait()
                    chain.link(dve.reciprocal(over, over))
                    for i in range(S.n):
                        chain.done(dve.tensor_scalar(x[:, i, :], x[:, i, :], den[:, b, i:i + 1], None, ALU.mult))
                    chain.wait()
                    dve.tensor_scalar(hmin[:, b, 0:S.n], x, 0.0, None, ALU.min).then_inc(s_hmin, 1)

                def add_residual(p, S, b):
                    x = num[:, b, 0:S.n]
                    dve.wait_ge(s_em, layer * NP + p + 1)
                    chain.link(dve.scalar_tensor_tensor(x, x, 0.0, hmin[:, b, 0:S.n], ALU.max, ALU.add))
                    dve.wait_ge(s_xres[b], 16 * (layer * (NP // 2) + p // 2 + 1))
                    if layer or not isinstance(p, int) or p > 1:
                        dve.wait_ge(s_out[b], 16 * (layer * (NP // 2) + p // 2))
                    dve.scalar_tensor_tensor(obuf[:, b, 0:S.n], x, -1.0, xres[:, b, 0:S.n], ALU.add, ALU.add).then_inc(s_fin, 1)

                def body(p, S, r, b):
                    r1, b1, later = (r - 1) % RING, 1 - b, not (isinstance(p, int) and p == 0)
                    S1 = Tiles(p - 1) if later else None
                    mask_and_max(p, S, r, b, 0)
                    if later:
                        normalise(S1, r1, b1)
                    row_max(S, r, b, True)
                    if later:
                        add_residual(p - 1, S1, b1)
                    less_max(S, r, b)
                    n = dve.value_load(nset[0:1, bass.ds(p, 1)], min_val=1, max_val=T)
                    chain.restart()
                    if T > S.G:
                        with dve.If(n > S.G):
                            with dve.Fori(1, (n + S.G - 1) // S.G) as g:
                                accumulate(S, r, b)
                                mask_and_max(p, S, r, b, g)
                                row_max(S, r, b, False)
                                less_max(S, r, b, True)
                                chain.restart()

                each_set(dve, body)
                S = Tiles(NP - 1)
                normalise(S, (NP - 1) % RING, (NP - 1) % 2)
                add_residual(NP - 1, S, (NP - 1) % 2)
                chain.restart()

            credit(dve, *s_h, *s_cen, *s_conv, *s_code, s_fin, s_fin)
            init()
            layernorm(0)
            value_sums(0)
            dve.wait_ge(s_slots, 2)
            pack()
            attend(0)
            layernorm(1)
            value_sums(1)
            attend(1)

        @block.tensor
        def _(pe):
            unit = registers(pe, "pe_unit", 1)
            deal, turn = registers(pe, "pe_deal", 1)[0:2]

            def weights():
                pe.wait_ge(s_const, 16 * CONSTANTS)
                pe.wait_ge(s_memset, 1)
                pe.wait_ge(s_W, 16 * 4)
                for l in range(2):
                    if l:
                        pe.wait_ge(s_was, 2 * l)
                    pe.transpose(ps[:, 0, 0:P], Wx[l][:, 0:F], ident[:, :]).then_inc(s_wt, 1)
                    pe.wait_ge(s_wts, l + 1)
                    pe.matmul(ps[:, 1, 0:2], WT[:, :], acol[l][:, :], start=True, stop=True).then_inc(s_wa, 1)
                pe.wait_ge(s_was, 4)

            def project(layer):
                def transposes(cc, b):
                    c = layer * NC2 + cc
                    pe.wait_ge(s_h[b], c + 2)
                    pe.wait_ge(s_hTs[b], c + 1)
                    for q in range(CH):
                        ins = pe.transpose(ps[:, b, q * P:(q + 1) * P], hrow[:, b, q, :], ident[:, :])
                    ins.then_inc(s_hT[b], 1)

                def products(cc, b):
                    c = layer * NC2 + cc
                    pe.wait_ge(s_hTs[b], c + 2)
                    pe.wait_ge(s_vrow[b], c + 1)
                    for q in range(CH):
                        ins = pe.matmul(ps[:, 2 + 2 * b + q // 2, (q % 2) * 256:(q % 2) * 256 + F + 2],
                                        hT[:, b, q * P:(q + 1) * P], Wx[layer][:, :], start=True, stop=True)
                    ins.then_inc(s_wh[b], 1)

                transposes(0, 0)
                with pe.Fori(0, NC2 - 1) as cc:
                    transposes(cc, 1)
                    products(cc, 0)
                    transposes(cc + 1, 0)
                    products(cc, 1)
                transposes(NC2 - 1, 1)
                products(NC2 - 1, 0)
                products(NC2 - 1, 1)
                for b in range(2):
                    pe.wait_ge(s_vs[b], NC2 * (layer + 1) + 1)
                for q in range(CH):
                    ins = pe.matmul(ps[:, 7, 0:VW], ones[:, :], vsum[:, q, 0:VW], start=(q == 0), stop=(q == CH - 1))
                ins.then_inc(s_sum, 1)
                pe.wait_ge(s_sumrep, layer + 1)

            def pack():
                def words_of(t, b):
                    third = not isinstance(t, int) or t > 1
                    if third:
                        deal_out()
                    pe.wait_ge(s_code[b], t // 2 + 1)
                    for k in range(LD):
                        pe.wait_ge(s_conv[k], t + 2)
                        for c in range(LB):
                            at = (k * LB + c) * NW
                            ins = pe.matmul(ps[:, b, at:at + NW], a01[:, k, c * P:(c + 1) * P], code[:, :],
                                            start=True, stop=True)
                        ins.then_inc(s_pack[k], 1)
                        if k == 0 and (third or t == 1):
                            counts_of(t - 1, 1 - b)
                        if k == 0 and third:
                            further_deals(t - 2)

                def counts_of(t, b):
                    pe.wait_ge(s_cnt, t + 1)
                    n = cnt[:, b:b + 1]
                    pe.transpose(ps[0:1, 2 + b, 0:P], n, ident[:, :])
                    pe.matmul(ps[:, 2 + b, P:P + 1], lanes_before[:, :], n, start=True, stop=True)
                    pe.matmul(ps[0:1, 2 + b, P + 1:P + 2], n, ones[:, 0:1], start=True, stop=True).then_inc(s_cntT[b], 1)

                def deal_out():
                    d, u = pe.snap(deal), pe.snap(turn)
                    pe.wait_ge(s_items, d)
                    pe.wait_ge(s_lane, u)
                    for s in range(FIND):
                        ins = pe.matmul(ps[:, 4, 0:DEAL * PW], at_lane[:, s, :], items[:, s].rearrange("p d w -> p (d w)"),
                                        start=(s == 0), stop=(s == FIND - 1))
                    ins.then_inc(s_dealt, 1)
                    pe.reg_add(deal, deal, 1)

                def further_deals(t):
                    if T <= min(FIND, DEAL):
                        pe.reg_add(turn, turn, 1)
                        return
                    n = pe.value_load(load[0:1, bass.ds(t, 1)], min_val=0, max_val=2 * T)
                    with pe.If(n > FIND):
                        rounds = (pe.value_load(nfind[0:1, bass.ds(t, 1)], min_val=0, max_val=T) + FIND - 1) // FIND
                        deals = (pe.value_load(nslots[0:1, bass.ds(t, 1)], min_val=1, max_val=T) + DEAL - 1) // DEAL
                        with pe.If(deals > 1):
                            with pe.Fori(1, deals):
                                deal_out()
                        pe.reg_add(turn, turn, 1)
                        if T > FIND:
                            with pe.If(rounds > 1):
                                with pe.Fori(1, rounds):
                                    with pe.Fori(0, deals):
                                        deal_out()
                                    pe.reg_add(turn, turn, 1)
                    with pe.Else():
                        pe.reg_add(turn, turn, 1)

                words_of(0, 0)
                words_of(1, 1)
                with pe.Fori(0, T2 - 1) as j:
                    for i in (2, 3):
                        words_of(2 * j + i, i % 2)
                deal_out()
                further_deals(T - 2)
                counts_of(T - 1, 1)
                deal_out()
                further_deals(T - 1)

            def attend(layer):
                def group(S, r, b, first_of=None):
                    u = pe.snap(unit[r])
                    if first_of is not None and not (isinstance(first_of, int) and first_of == NP - 1):
                        spread_query(first_of + 1, 1 - b)
                    pe.wait_ge(s_kr[r], u)
                    for i in range(S.n):
                        ins = pe.transpose(kT[b][:, i, :], kr[:, b, i, :], ident[:, :])
                    ins.then_inc(s_kT[r], 1)
                    pe.wait_ge(s_mb[r], u)
                    for i in range(S.n):
                        ins = pe.matmul(mrep[b][:, i, :], mb[:, b, i, :], ident[:, :], start=True, stop=True)
                    ins.then_inc(s_mrep[r], 1)
                    pe.wait_ge(s_p[r], u)
                    weights = S.cells(pr[:, b])
                    for i in range(S.n):
                        for s in range(S.G):
                            ins = pe.matmul(prod[b][:, i, :], weights[:, i, s, :], rows[:, r, i * S.G + s, 0:VW],
                                            start=(s == 0), stop=(s == S.G - 1))
                    ins.then_inc(s_pv[r], 1)
                    pe.reg_add(unit[r], unit[r], 1)

                def spread_query(p, b):
                    pe.wait_ge(s_qb, layer * NP + p + 1)
                    for i in range(Tiles(p).n):
                        ins = pe.matmul(qrep[b][:, i, :], qb[:, b, i, :], ident[:, :], start=True, stop=True)
                    ins.then_inc(s_qrep, 1)

                def body(p, S, r, b):
                    if isinstance(p, int) and p == 0:
                        spread_query(0, 0)
                    group(S, r, b, p)
                    if T > S.G:
                        n = pe.value_load(nset[0:1, bass.ds(p, 1)], min_val=1, max_val=T)
                        with pe.If(n > S.G):
                            with pe.Fori(1, (n + S.G - 1) // S.G) as g:
                                group(S, r, b)

                each_set(pe, body)

            credit(pe, *s_hT, *s_pack, *s_pv)
            weights()
            project(0)
            pack()
            attend(0)
            project(1)
            attend(1)


def kernel(x, adj, L0_gnn_W, L0_gnn_a, L1_gnn_W, L1_gnn_a):
    import concourse.bacc as bacc
    from concourse.bass_utils import run_bass_kernel_spmd

    x, adj = np.ascontiguousarray(x), np.ascontiguousarray(adj)
    T = x.shape[0] // P
    i = np.arange(P)
    code = np.where(i[:, None] // WORD == np.arange(NW)[None, :], 2.0 ** (i[:, None] % WORD), 0.0).astype(np.float32)
    arrays = {
        "in_x": x, "in_adj": adj,
        "in_W0": np.ascontiguousarray(L0_gnn_W), "in_a0": np.ascontiguousarray(L0_gnn_a),
        "in_W1": np.ascontiguousarray(L1_gnn_W), "in_a1": np.ascontiguousarray(L1_gnn_a).reshape(-1),
        "c_ident": np.eye(P, dtype=np.float32),
        "c_code": code,
        "c_bitmask": np.broadcast_to((1 << (i % WORD)).astype(np.uint16), (P, P)).copy(),
        "c_block": np.broadcast_to(((np.arange(T) + 1) * BLOCK_CODE).astype(np.float32), (P, T)).copy(),
        "c_lane": (i - P).astype(np.float32).reshape(P, 1),
        "c_iota": np.broadcast_to(i.astype(np.float32), (P, P)).copy(),
        "c_before": (i[:, None] < i[None, :]).astype(np.float32),
    }
    nc = bacc.Bacc("TRN2", target_bir_lowering=False, num_devices=1)
    args = [nc.dram_tensor(k, a.shape, mybir.dt.from_np(a.dtype), kind="ExternalInput").ap() for k, a in arrays.items()]
    out = nc.dram_tensor("out_x", x.shape, F32, kind="ExternalOutput").ap()
    gat_two_layers(nc, *args, out)
    return run_bass_kernel_spmd(nc, [arrays], core_ids=[0]).results[0]["out_x"]
```
